# Optimizing a Trainium2 kernel written in Bass

```python
import numpy as np
import jax
import jax.numpy as jnp

def _softmax(x, axis=-1):
    return jax.nn.softmax(x, axis=axis)

def _gelu(x):
    return jax.nn.gelu(x, approximate=True)

def _silu(x):
    return jax.nn.silu(x)

def _sigmoid(x):
    return jax.nn.sigmoid(x)

def _layernorm(x, axis=-1, eps=1e-05):
    m = jnp.mean(x, axis=axis, keepdims=True)
    v = jnp.var(x, axis=axis, keepdims=True)
    return (x - m) / jnp.sqrt(v + eps)

def _scatter_add(tgt, idx, src, axis=0):
    return tgt.at[idx].add(src)

def _segment_sum(src, seg, n):
    return jax.ops.segment_sum(src, seg, n)
kernel_name = 'mk_flamingo_gated_d2_seqx_r4_e5627a'

def setup_inputs(seed: int=0):
    np.random.seed(seed)
    _w = jnp.asarray

    def _rec_inputs():
        import jax
        import jax.numpy as jnp
        _rk = jax.random.key(seed)
        x = -0.000125 + 0.9999 * jax.random.normal(jax.random.fold_in(_rk, 1), (4, 512, 512), jnp.float32)
        _lenS = 512 - jax.random.randint(jax.random.fold_in(_rk, 7), (4,), 0, max(1, 512 // 4) + 1, jnp.int32)
        _lenS2 = 1024 - jax.random.randint(jax.random.fold_in(_rk, 8), (4,), 0, max(1, 1024 // 4) + 1, jnp.int32)
        _ctx_2048P = jax.random.normal(jax.random.fold_in(_rk, 11), (4, 16, 512), jnp.float32)
        _ctx_2048c = jax.random.dirichlet(jax.random.fold_in(_rk, 511), 0.3 * jnp.ones((16,), jnp.float32), (4, 1024))
        _ctx_2048t = jnp.einsum('bsk,bkd->bsd', _ctx_2048c, _ctx_2048P)
        _ctx_2048t = _ctx_2048t * jax.lax.rsqrt(jnp.mean(jnp.square(_ctx_2048t)) + 1e-12) * 0.953939
        ctx_2048 = -0.000514642 + 1.00011 * (_ctx_2048t + 0.3 * jax.random.normal(jax.random.fold_in(_rk, 611), (4, 1024, 512), jnp.float32))
        _validS = jnp.arange(512)[None, :] < _lenS[:, None]
        _validS2 = jnp.arange(1024)[None, :] < _lenS2[:, None]
        _causal = jnp.tril(jnp.ones((512, 512), dtype=bool))
        mask_BxS2_bk0 = jnp.logical_not(jnp.broadcast_to(_validS2[:, :], (4, 1024)))
        _g = jax.random.normal(jax.random.fold_in(_rk, 9001), (2, 2), jnp.float32)
        _g = jnp.sign(_g) * jnp.maximum(jnp.abs(_g), 1.0) + (_g == 0) * 1.0
        g_xattn = _g[0]
        g_ffn = _g[1]
        return (x, ctx_2048, mask_BxS2_bk0, g_xattn, g_ffn)
    x, ctx_2048, mask_BxS2_bk0, g_xattn, g_ffn = _rec_inputs()

    def _L0_xattn_setup():
        import jax, jax.numpy as jnp
        import numpy as np
        key = jax.random.key(seed)
        k1, k2, k3 = jax.random.split(key, 3)
        B, S, D, M = (8, 512, 512, 128)
        hidden_states = jax.random.normal(k1, (B, S, D), dtype=jnp.float32)
        memory_tokens = jax.random.normal(k2, (B, M, D), dtype=jnp.float32)
        memory_mask = jax.random.randint(k3, (B, M), 0, 2).astype(jnp.bool_)
        return {'hidden_states': hidden_states, 'memory_tokens': memory_tokens, 'memory_mask': memory_mask}
    _L0_xattn_all = _L0_xattn_setup()
    _L0_xattn_in = {k: v for k, v in _L0_xattn_all.items() if k in ()}
    del _L0_xattn_all

    def _L0_ffn_setup():
        import jax, jax.numpy as jnp
        import numpy as np
        EPS = 1e-05

        def _weight_quant(w):
            s = 1.0 / jnp.clip(jnp.mean(jnp.abs(w)), EPS, None)
            return jnp.clip(jnp.round(w * s), -1.0, 1.0) / s

        def _act_quant(x):
            s = 127.0 / jnp.clip(jnp.max(jnp.abs(x), axis=-1, keepdims=True), EPS, None)
            return jnp.clip(jnp.round(x * s), -128.0, 127.0) / s

        def bitlinear(x, w):
            wq = w + jax.lax.stop_gradient(_weight_quant(w) - w)
            xq = x + jax.lax.stop_gradient(_act_quant(x) - x)
            return xq @ wq.T
        key = jax.random.key(seed)
        k = jax.random.split(key, 5)
        B, S, H, E, D = (4, 1024, 512, 8, 512)
        x = jax.random.normal(k[0], (B, S, H), dtype=jnp.float32)
        router_w = jax.random.normal(k[1], (E, H), dtype=jnp.float32) * 0.02
        wg = jax.random.normal(k[2], (E, D, H), dtype=jnp.float32) * 0.02
        wu = jax.random.normal(k[3], (E, D, H), dtype=jnp.float32) * 0.02
        wd = jax.random.normal(k[4], (E, H, D), dtype=jnp.float32) * 0.02
        return {'x': x, 'router_w': router_w, 'wg': wg, 'wu': wu, 'wd': wd}
    _L0_ffn_all = _L0_ffn_setup()
    _L0_ffn_in = {k: v for k, v in _L0_ffn_all.items() if k in ('router_w', 'wg', 'wu', 'wd')}
    del _L0_ffn_all

    def _L1_xattn_setup():
        import jax, jax.numpy as jnp
        import numpy as np
        D_MODEL = 512
        NUM_HEADS = 16
        HEAD_DIM = D_MODEL // NUM_HEADS
        key = jax.random.key(seed)
        ks = jax.random.split(key, 10)
        B, S, T = (4, 1024, 256)
        s = 1.0 / np.sqrt(D_MODEL)
        inp = {'query': jax.random.normal(ks[0], (B, S, D_MODEL), jnp.float32), 'key_value': jax.random.normal(ks[1], (B, T, D_MODEL), jnp.float32), 'Wq': jax.random.normal(ks[2], (D_MODEL, D_MODEL), jnp.float32) * s, 'bq': jnp.zeros((D_MODEL,), jnp.float32), 'Wk': jax.random.normal(ks[3], (D_MODEL, D_MODEL), jnp.float32) * s, 'bk': jnp.zeros((D_MODEL,), jnp.float32), 'Wv': jax.random.normal(ks[4], (D_MODEL, D_MODEL), jnp.float32) * s, 'bv': jnp.zeros((D_MODEL,), jnp.float32), 'Wo': jax.random.normal(ks[5], (D_MODEL, D_MODEL), jnp.float32) * s, 'bo': jnp.zeros((D_MODEL,), jnp.float32)}
        return inp
    _L1_xattn_all = _L1_xattn_setup()
    _L1_xattn_in = {k: v for k, v in _L1_xattn_all.items() if k in ('Wq', 'bq', 'Wk', 'bk', 'Wv', 'bv', 'Wo', 'bo')}
    del _L1_xattn_all

    def _L1_ffn_setup():
        import jax, jax.numpy as jnp
        import numpy as np
        E, D_MODEL, D_FF = (8, 512, 2048)
        B, CAP = (4, 256)
        key = jax.random.key(seed)
        k_x, k_w1, k_w2 = jax.random.split(key, 3)
        scale = 0.02
        x = jax.random.normal(k_x, (B, E * CAP, D_MODEL), dtype=jnp.float32)
        w1 = jax.random.normal(k_w1, (E, D_MODEL, D_FF), dtype=jnp.float32) * scale
        b1 = jnp.zeros((E, D_FF), dtype=jnp.float32)
        w2 = jax.random.normal(k_w2, (E, D_FF, D_MODEL), dtype=jnp.float32) * scale
        b2 = jnp.zeros((E, D_MODEL), dtype=jnp.float32)
        return {'x': x, 'w1': w1, 'b1': b1, 'w2': w2, 'b2': b2}
    _L1_ffn_all = _L1_ffn_setup()
    _L1_ffn_in = {k: v for k, v in _L1_ffn_all.items() if k in ('w1', 'b1', 'w2', 'b2')}
    del _L1_ffn_all
    return {'x': x, 'ctx_2048': ctx_2048, 'mask_BxS2_bk0': mask_BxS2_bk0, 'g_xattn': g_xattn, 'g_ffn': g_ffn, 'L0_ffn_router_w': _L0_ffn_in['router_w'], 'L0_ffn_wg': _L0_ffn_in['wg'], 'L0_ffn_wu': _L0_ffn_in['wu'], 'L0_ffn_wd': _L0_ffn_in['wd'], 'L1_xattn_Wq': _L1_xattn_in['Wq'], 'L1_xattn_bq': _L1_xattn_in['bq'], 'L1_xattn_Wk': _L1_xattn_in['Wk'], 'L1_xattn_bk': _L1_xattn_in['bk'], 'L1_xattn_Wv': _L1_xattn_in['Wv'], 'L1_xattn_bv': _L1_xattn_in['bv'], 'L1_xattn_Wo': _L1_xattn_in['Wo'], 'L1_xattn_bo': _L1_xattn_in['bo'], 'L1_ffn_w1': _L1_ffn_in['w1'], 'L1_ffn_b1': _L1_ffn_in['b1'], 'L1_ffn_w2': _L1_ffn_in['w2'], 'L1_ffn_b2': _L1_ffn_in['b2']}

def reference(x, ctx_2048, mask_BxS2_bk0, g_xattn, g_ffn, L0_ffn_router_w, L0_ffn_wg, L0_ffn_wu, L0_ffn_wd, L1_xattn_Wq, L1_xattn_bq, L1_xattn_Wk, L1_xattn_bk, L1_xattn_Wv, L1_xattn_bv, L1_xattn_Wo, L1_xattn_bo, L1_ffn_w1, L1_ffn_b1, L1_ffn_w2, L1_ffn_b2):
    import jax
    import jax.numpy as jnp

    def _L0_xattn_ref(hidden_states, memory_tokens, memory_mask):
        import jax, jax.numpy as jnp
        import numpy as np
        B, S, D = hidden_states.shape
        scale = 1.0 / jnp.sqrt(jnp.asarray(D, hidden_states.dtype))
        scores = jnp.einsum('bsd,bmd->bsm', hidden_states, memory_tokens) * scale
        neg_inf = jnp.asarray(-1e+30, scores.dtype)
        scores = jnp.where(memory_mask[:, None, :], scores, neg_inf)
        attn = jax.nn.softmax(scores, axis=-1)
        readout = jnp.einsum('bsm,bmd->bsd', attn, memory_tokens)
        valid_b = jnp.any(memory_mask, axis=-1)
        out = jnp.where(valid_b[:, None, None], readout, jnp.zeros_like(readout))
        return out

    def _L0_ffn_ref(x, router_w, wg, wu, wd):
        import jax, jax.numpy as jnp
        import numpy as np
        EPS = 1e-05

        def _weight_quant(w):
            s = 1.0 / jnp.clip(jnp.mean(jnp.abs(w)), EPS, None)
            return jnp.clip(jnp.round(w * s), -1.0, 1.0) / s

        def _act_quant(x):
            s = 127.0 / jnp.clip(jnp.max(jnp.abs(x), axis=-1, keepdims=True), EPS, None)
            return jnp.clip(jnp.round(x * s), -128.0, 127.0) / s

        def bitlinear(x, w):
            wq = w + jax.lax.stop_gradient(_weight_quant(w) - w)
            xq = x + jax.lax.stop_gradient(_act_quant(x) - x)
            return xq @ wq.T
        B, S, H = x.shape
        E = wg.shape[0]
        logits = jnp.einsum('bsh,eh->bse', x, router_w)
        idx = jnp.argmax(logits, axis=-1).reshape(-1)
        xf = x.reshape(-1, H)
        out = jnp.zeros_like(xf)
        for e in range(E):
            g = bitlinear(xf, wg[e])
            u = bitlinear(xf, wu[e])
            y = bitlinear(jnp.square(jax.nn.relu(g)) * u, wd[e])
            out = out + jnp.where((idx == e)[:, None], y, 0.0)
        return out.reshape(B, S, H)

    def _L1_xattn_ref(query, key_value, Wq, bq, Wk, bk, Wv, bv, Wo, bo):
        import jax, jax.numpy as jnp
        import numpy as np
        D_MODEL = 512
        NUM_HEADS = 16
        HEAD_DIM = D_MODEL // NUM_HEADS
        B, S, _ = query.shape
        T = key_value.shape[1]
        Q = query @ Wq.T + bq
        K = key_value @ Wk.T + bk
        V = key_value @ Wv.T + bv
        Q = Q.reshape(B, S, NUM_HEADS, HEAD_DIM).transpose(0, 2, 1, 3)
        K = K.reshape(B, T, NUM_HEADS, HEAD_DIM).transpose(0, 2, 1, 3)
        V = V.reshape(B, T, NUM_HEADS, HEAD_DIM).transpose(0, 2, 1, 3)
        scale = 1.0 / np.sqrt(HEAD_DIM).astype(np.float32)
        scores = jnp.einsum('bhsd,bhtd->bhst', Q, K) * scale
        attn = jax.nn.softmax(scores, axis=-1)
        ctx = jnp.einsum('bhst,bhtd->bhsd', attn, V)
        ctx = ctx.transpose(0, 2, 1, 3).reshape(B, S, D_MODEL)
        return ctx @ Wo.T + bo

    def _L1_ffn_ref(x, w1, b1, w2, b2):
        import jax, jax.numpy as jnp
        import numpy as np
        E, D_MODEL, D_FF = (8, 512, 2048)
        B, CAP = (4, 256)
        Bsz, T, d = x.shape
        nE = w1.shape[0]
        cap = T // nE
        xe = x.reshape(Bsz, nE, cap, d)
        h = jnp.einsum('becd,edf->becf', xe, w1) + b1[:, None, :]
        h = jax.nn.gelu(h, approximate=False)
        out = jnp.einsum('becf,efd->becd', h, w2) + b2[:, None, :]
        return out.reshape(Bsz, T, d)
    x = x + jnp.tanh(g_xattn[0]) * _L0_xattn_ref(_layernorm(x, axis=-1), ctx_2048, mask_BxS2_bk0)
    x = x + jnp.tanh(g_ffn[0]) * _L0_ffn_ref(_layernorm(x, axis=-1), L0_ffn_router_w, L0_ffn_wg, L0_ffn_wu, L0_ffn_wd)
    x = x + jnp.tanh(g_xattn[1]) * _L1_xattn_ref(_layernorm(x, axis=-1), ctx_2048, L1_xattn_Wq, L1_xattn_bq, L1_xattn_Wk, L1_xattn_bk, L1_xattn_Wv, L1_xattn_bv, L1_xattn_Wo, L1_xattn_bo)
    x = x + jnp.tanh(g_ffn[1]) * _L1_ffn_ref(_layernorm(x, axis=-1), L1_ffn_w1, L1_ffn_b1, L1_ffn_w2, L1_ffn_b2)
    return x

_drawn_inputs = setup_inputs


def setup_inputs(seed=0):
    import zlib

    import numpy as np

    out = dict(_drawn_inputs(seed))
    spreads = {'g_ffn': (-1.0, 0.6),
     'L1_xattn_bq': (0.0, 2.0),
     'L1_xattn_bk': (0.0, 2.0),
     'L1_xattn_bv': (0.0, 0.8),
     'L1_xattn_bo': (0.0, 2.0),
     'L1_ffn_b1': (0.0, 0.8),
     'L1_ffn_b2': (0.0, 2.0)}
    factors = {'L0_ffn_router_w': 8.0,
     'L0_ffn_wg': 8.0,
     'L0_ffn_wu': 8.0,
     'L0_ffn_wd': 8.0,
     'L1_xattn_Wq': 8.0,
     'L1_xattn_Wk': 8.0,
     'L1_xattn_Wv': 3.311,
     'L1_xattn_Wo': 3.218,
     'L1_ffn_w1': 8.0,
     'L1_ffn_w2': 7.728}
    for name, (base, spread) in spreads.items():
        noise = np.random.default_rng([zlib.crc32(name.encode()), seed]).standard_normal(out[name].shape)
        drawn = base * np.exp(spread * noise) if base else spread * noise
        out[name] = jnp.asarray(drawn.astype(out[name].dtype))
    for name, factor in factors.items():
        out[name] = (out[name] * factor).astype(out[name].dtype)
    return out
```

```python
from contextlib import ExitStack

import concourse.bass as bass
from concourse import mybir

F32 = mybir.dt.float32
BF16 = mybir.dt.bfloat16
ACT = mybir.ActivationFunctionType
ALU = mybir.AluOpType
AX_X = mybir.AxisListType.X

P = 128
B, S, D = 4, 512, 512
T = 1024
KC = D // P
NH, HD = 16, 32
VW = 3 * HD
E = 8
NT = B * S // P
EPS = 1e-5
MAGIC = 1.5 * 2.0 ** 23
DW = D + 8
QD = 4


def three_products(a_hi, a_lo, b_hi, b_lo):
    return ((a_hi, b_hi), (a_hi, b_lo), (a_lo, b_hi))


def context_phase(nc, sem, ctx, wk, bk, wv, keys_dram, values_dram, ident, ctxN, ctxT, x, xres, moments,
                  gate_x, gate_f, gates):
    NQ = B * T // (QD * P)
    ctx_v = ctx.rearrange("b (h u p) d -> (b h) p u d", u=QD, p=P)
    keys_v = keys_dram.rearrange("q r (c p) t -> q c p r t", p=P)
    values_v = values_dram.rearrange("b (h u p) n -> (b h) u p n", u=QD, p=P)
    with ExitStack() as c:
        sb = lambda name, shape, dt: c.enter_context(nc.sbuf_tensor(name, shape, dt))
        rows32 = sb("c_rows32", [P, 2, QD, D], F32)
        wT = sb("c_wT", [P, 2, 2 * KC, D], BF16)
        bias = sb("c_bias", [P, KC], F32)
        kst = sb("c_kst", [P, 2, 2, 512], BF16)
        vst = sb("c_vst", [P, 2, NH, VW], BF16)
        psT = c.enter_context(nc.psum_tensor("c_psT", [P, 2, 2 * KC, P], BF16))
        psG = c.enter_context(nc.psum_tensor("c_psG", [P, 4, 512], F32))
        rows_loaded = [sem(f"c_rows_loaded{i}") for i in range(2)]
        bias_loaded = sem("c_bias_loaded")
        hi_done = sem("c_hi_done")
        lo_done = sem("c_lo_done")
        xposed = sem("c_xposed")
        even_copied = sem("c_even_copied")
        odd_copied = sem("c_odd_copied")
        gemm_done = sem("c_gemm_done")
        hi_out = sem("c_hi_out")
        lo_out = sem("c_lo_out")
        ones_set = sem("c_ones_set")
        ident_zero, ident_ready = sem("c_ident_zero"), sem("c_ident_ready")
        x_loaded = [sem(f"c_x_loaded{i}") for i in range(B)]
        x_stats = sem("c_x_stats")
        x_moments = sem("c_x_moments")
        stats = sb("c_stats", [P, NT, 6], F32)
        gates_loaded, tanh_done = sem("c_gates_loaded"), sem("c_tanh_done")
        raw_gates = sb("c_raw_gates", [P, 4], F32)
        k_stored = [sem(f"c_k_stored{i}") for i in range(2)]
        v_stored = [sem(f"c_v_stored{i}") for i in range(2)]

        with nc.Block() as block:
            @block.gpsimd
            def _(pool):
                nc.gpsimd.memset(ident[:, :], 0.0).then_inc(ident_zero, 1)
                pool.wait_ge(ident_zero, 1)
                nc.gpsimd.affine_select(out=ident[:, :], in_=ident[:, :], compare_op=ALU.not_equal, fill=1.0,
                                        base=0, pattern=[[-1, P]], channel_multiplier=1).then_inc(ident_ready, 1)
                nc.gpsimd.memset(vst[:, :, :, 2 * HD:VW], 1.0).then_inc(ones_set, 1)

            @block.sync
            def _(sp):
                def load(j, slot, src):
                    sp.dma_start(rows32[:, slot, :, :], src).then_inc(rows_loaded[slot], 16)

                def store(q):
                    for k in range(QD):
                        sp.wait_ge(lo_out, q * 8 + k + 5)
                        sp.dma_start(keys_v[bass.ds(q, 1), k].rearrange("o p r t -> p (o r) t"),
                                     kst[:, k % 2, :, :]).then_inc(k_stored[k % 2], 16)
                    for k in range(QD):
                        sp.wait_ge(lo_out, q * 8 + k + 9)
                        sp.dma_start(values_v[bass.ds(q, 1), k].rearrange("o p n -> p (o n)"),
                                     vst[:, k % 2, :, :].rearrange("p h w -> p (h w)")).then_inc(v_stored[k % 2], 16)

                def load_ctx(j, slot):
                    sp.wait_ge(lo_done, (j - 1) * QD)
                    load(j, slot, ctx_v[bass.ds(j - 2, 1)].rearrange("o p u d -> p (o u) d"))

                for k in range(2):
                    sp.sem_inc(k_stored[k], 16)
                    sp.sem_inc(v_stored[k], 16)
                load(0, 0, wk.rearrange("(u p) d -> p u d", p=P))
                load(1, 1, wv.rearrange("(u p) d -> p u d", p=P))
                sp.dma_start(bias[:, :], bk.rearrange("(c p) -> p c", p=P),
                             allow_slow_non_contiguous=True).then_inc(bias_loaded, 16)
                for i, g in enumerate((gate_x, gate_f)):
                    sp.dma_start(raw_gates[:, 2 * i:2 * i + 2],
                                 g.rearrange("(o n) -> o n", o=1).to_broadcast([P, 2])).then_inc(gates_loaded, 16)
                for j in (2, 3, 4):
                    load_ctx(j, j % 2)
                for b in range(B):
                    sp.dma_start(xres[:, 4 * b:4 * b + 4, :],
                                 x[b].rearrange("(u p) d -> p u d", p=P)).then_inc(x_loaded[b], 16)
                with sp.Fori(0, 2) as i:
                    q = 2 * i
                    load_ctx(q + 5, 1)
                    store(q)
                    load_ctx(q + 6, 0)
                    store(q + 1)
                load_ctx(9, 1)
                with sp.Fori(4, NQ) as q:
                    store(q)
                for k in range(2):
                    sp.wait_ge(k_stored[k], 16 * (2 * NQ + 1))
                    sp.wait_ge(v_stored[k], 16 * (2 * NQ + 1))

            def split_views(j, par, u):
                t = (j + 6) * QD + u if isinstance(j, int) and j < 2 else (j - 2) * QD + u
                return (ctxN[:, bass.ds(t, 1), 0, :].rearrange("p o d -> p (o d)"),
                        ctxN[:, bass.ds(t, 1), 1, :].rearrange("p o d -> p (o d)"))

            def copy_view(j, u):
                if isinstance(j, int) and j < 2:
                    return wT[:, j, :, u * P:(u + 1) * P]
                return ctxT[:, :, bass.ds(((j - 2) * QD + u) * P, P)]

            @block.scalar
            def _(act):
                def split(j, par):
                    act.wait_ge(rows_loaded[par], (j // 2 + 1) * 16)
                    for u in range(QD):
                        nc.scalar.copy(split_views(j, par, u)[0], rows32[:, par, u, :]).then_inc(hi_done, 1)

                def copy(j):
                    for u in (0, 2):
                        act.wait_ge(xposed, j * QD + u + 1)
                        nc.scalar.copy(copy_view(j, u), psT[:, 0, :, :]).then_inc(even_copied, 1)

                def evacuate(q):
                    for k in range(QD):
                        act.wait_ge(gemm_done, q * 8 + k + 1)
                        act.wait_ge(k_stored[k % 2], q * 32 + k // 2 * 16 + 16)
                        nc.scalar.activation(kst[:, k % 2, 0, :], psG[:, k, :], ACT.Identity,
                                             bias=bias[:, k:k + 1]).then_inc(hi_out, 1)
                    for k in range(QD):
                        act.wait_ge(gemm_done, q * 8 + k + 5)
                        act.wait_ge(v_stored[k % 2], q * 32 + k // 2 * 16 + 16)
                        nc.scalar.copy(vst[:, k % 2, :, 0:HD],
                                       psG[:, k, :].rearrange("p (h w) -> p h w", h=NH)).then_inc(hi_out, 1)

                act.sem_inc(even_copied, 1)
                act.wait_ge(bias_loaded, 16)
                act.wait_ge(ones_set, 1)
                split(0, 0)
                split(1, 1)
                copy(0)
                split(2, 0)
                copy(1)
                split(3, 1)
                copy(2)
                with act.Fori(0, 3) as i:
                    for par in (0, 1):
                        q = 2 * i
                        copy(q + par + 3)
                        split(q + par + 4, par)
                        evacuate(q + par)
                copy(9)
                evacuate(6)
                evacuate(7)
                act.wait_ge(gates_loaded, 32)
                nc.scalar.activation(gates[:, :], raw_gates[:, :], ACT.Tanh).then_inc(tanh_done, 1)

            @block.vector
            def _(dve):
                def split(j, par):
                    for u in range(QD):
                        dve.wait_ge(hi_done, j * QD + u + 1)
                        hi, lo = split_views(j, par, u)
                        nc.vector.tensor_tensor(lo, rows32[:, par, u, :], hi, ALU.subtract).then_inc(lo_done, 1)

                def copy(j):
                    for u in (1, 3):
                        dve.wait_ge(xposed, j * QD + u + 1)
                        nc.vector.tensor_copy(copy_view(j, u), psT[:, 1, :, :]).then_inc(odd_copied, 1)

                def evacuate(q):
                    for k in range(QD):
                        dve.wait_ge(hi_out, q * 8 + k + 1)
                        nc.vector.scalar_tensor_tensor(kst[:, k % 2, 1, :], psG[:, k, :], bias[:, k:k + 1],
                                                       kst[:, k % 2, 0, :], ALU.add, ALU.subtract).then_inc(lo_out, 1)
                    for k in range(QD):
                        dve.wait_ge(hi_out, q * 8 + k + 5)
                        nc.vector.tensor_tensor(vst[:, k % 2, :, HD:2 * HD],
                                                psG[:, k, :].rearrange("p (h w) -> p h w", h=NH),
                                                vst[:, k % 2, :, 0:HD], ALU.subtract).then_inc(lo_out, 1)

                dve.sem_inc(odd_copied, 1)
                dve.sem_inc(lo_out, 4)
                dve.wait_ge(bias_loaded, 16)
                split(0, 0)
                split(1, 1)
                copy(0)
                split(2, 0)
                copy(1)
                split(3, 1)
                copy(2)
                with dve.Fori(0, 3) as i:
                    for par in (0, 1):
                        q = 2 * i
                        copy(q + par + 3)
                        split(q + par + 4, par)
                        evacuate(q + par)
                copy(9)
                for t in range(NT):
                    if t % QD == 0:
                        dve.wait_ge(x_loaded[t // QD], 16)
                    nc.vector.bn_stats(stats[:, t, :], xres[:, t, :]).then_inc(x_stats, 1)
                evacuate(6)
                evacuate(7)
                for t in range(NT):
                    dve.wait_ge(x_stats, t + 1)
                    nc.vector.bn_aggr(moments[:, t, :], stats[:, t, :]).then_inc(x_moments, 1)

            @block.tensor
            def _(pe):
                def prepare(j):
                    for u in range(QD):
                        pe.wait_ge(lo_done, j * QD + u + 1)
                        bank_free = even_copied if u % 2 == 0 else odd_copied
                        pe.wait_ge(bank_free, j * 2 + u // 2 + 1)
                        hi, lo = split_views(j, 0, u)
                        for r, half in enumerate((hi, lo)):
                            for k in range(KC):
                                last = nc.tensor.transpose(psT[:, u % 2, r * KC + k, :], half[:, k * P:(k + 1) * P],
                                                           ident[:, :])
                        last.then_inc(xposed, 1)

                def gemm(q):
                    pe.wait_ge(even_copied, 2 * q + 7)
                    pe.wait_ge(odd_copied, 2 * q + 7)
                    def pairs(a, b):
                        return [(a + k, b + k) for a, b in ((0, 0), (0, KC), (KC, 0)) for k in range(KC)]
                    for n in range(QD):
                        pe.wait_ge(lo_out, q * 8 + n + 1)
                        for i, (a, b) in enumerate(pairs(0, 0)):
                            last = nc.tensor.matmul(psG[:, n, :], wT[:, 0, a, n * P:(n + 1) * P],
                                                    ctxT[:, b, bass.ds(q * 512, 512)], start=(i == 0), stop=(i == 11))
                        last.then_inc(gemm_done, 1)
                    for n in range(QD):
                        pe.wait_ge(lo_out, q * 8 + n + 5)
                        for i, (a, b) in enumerate(pairs(0, 0)):
                            last = nc.tensor.matmul(psG[:, n, :], ctxT[:, a, bass.ds(q * 512 + n * P, P)],
                                                    wT[:, 1, b, :], start=(i == 0), stop=(i == 11))
                        last.then_inc(gemm_done, 1)

                pe.wait_ge(ident_ready, 1)
                prepare(0)
                prepare(1)
                prepare(2)
                with pe.Fori(0, 7) as q:
                    prepare(q + 3)
                    gemm(q)
                gemm(7)


def readout_phase(nc, sem, mask, gates, ident, ctxN, ctxT, xres, moments):
    SC = float(D) ** -0.5
    TC = T // P
    with ExitStack() as c:
        sb = lambda name, shape, dt: c.enter_context(nc.sbuf_tensor(name, shape, dt))
        mask8 = sb("a_mask8", [P, B, T], mybir.dt.uint8)
        maskb = sb("a_maskb", [P, B, T], BF16)
        anyb = sb("a_anyb", [P, B], F32)
        factor = sb("a_factor", [P, B], F32)
        half = sb("a_half", [P, NT], F32)
        veps = sb("a_veps", [P, NT], F32)
        rstd = sb("a_rstd", [P, NT], F32)
        xn = sb("a_xn", [P, D], F32)
        xpair = sb("a_xpair", [P, 2, 2, D], BF16)
        xT = sb("a_xT", [P, 2, 2 * KC, P], BF16)
        probs = sb("a_probs", [P, 2, T], F32)
        ppair = sb("a_ppair", [P, 2, 2, T], BF16)
        pT = sb("a_pT", [P, 2, 2 * TC, P], BF16)
        nmax = sb("a_nmax", [P, NT], F32)
        sums = sb("a_sums", [P, NT], F32)
        rsum = sb("a_rsum", [P, NT], F32)
        coef = sb("a_coef", [P, NT], F32)
        stats = sb("a_stats", [P, NT, 6], F32)
        psS = c.enter_context(nc.psum_tensor("a_psS", [P, 2, T], F32))
        psP = c.enter_context(nc.psum_tensor("a_psP", [P, 2, TC, P], BF16))
        psX = c.enter_context(nc.psum_tensor("a_psX", [P, 2 * KC, P], BF16))
        psR = c.enter_context(nc.psum_tensor("a_psR", [P, D], F32))
        mask_loaded = sem("a_mask_loaded")
        setup = sem("a_setup")
        rstd_ready = sem("a_rstd_ready")
        normed = sem("a_normed")
        xhi_done, xlo_done = sem("a_xhi_done"), sem("a_xlo_done")
        xposed = sem("a_xposed")
        xcopied = sem("a_xcopied")
        scored = sem("a_scored")
        masked = sem("a_masked")
        maxed = sem("a_maxed")
        expd = sem("a_expd")
        phi_done, plo_done = sem("a_phi_done"), sem("a_plo_done")
        pposed = sem("a_pposed")
        p_hi_copied = sem("a_p_hi_copied")
        p_lo_copied = sem("a_p_lo_copied")
        readout = sem("a_readout")
        rsum_ready, coef_ready = sem("a_rsum_ready"), sem("a_coef_ready")
        updated = sem("a_updated")
        stats_ready, moments_ready = sem("a_stats_ready"), sem("a_moments_ready")

        with nc.Block() as block:
            @block.sync
            def _(sp):
                sp.dma_start(mask8[:, :, :].rearrange("p b t -> p (b t)"),
                             mask.rearrange("(o b) t -> o (b t)", o=1).to_broadcast([P, B * T])).then_inc(mask_loaded, 16)

            @block.gpsimd
            def _(pool):
                nc.gpsimd.memset(half[:, :], -0.5).then_inc(rstd_ready, 1)
                nc.gpsimd.tensor_scalar(veps[:, :], moments[:, :, 1], EPS, None, ALU.add).then_inc(rstd_ready, 1)
                pool.wait_ge(rstd_ready, 2)
                nc.gpsimd.tensor_tensor(rstd[:, :], veps[:, :], half[:, :], ALU.pow).then_inc(rstd_ready, 1)

            @block.scalar
            def _(act):
                def x_hi(t, par):
                    act.wait_ge(normed, t + 1)
                    act.wait_ge(xposed, t + 1)
                    nc.scalar.copy(xpair[:, par, 0, :], xn[:, :]).then_inc(xhi_done, 1)

                def x_copy(t, par):
                    act.wait_ge(xposed, t + 3)
                    act.wait_ge(scored, t + 1)
                    nc.scalar.copy(xT[:, par, :, :], psX[:, :, :]).then_inc(xcopied, 1)

                def exponentials(t, par):
                    act.wait_ge(maxed, t + 1)
                    nc.scalar.activation(probs[:, par, :], probs[:, par, :], ACT.Exp,
                                         bias=nmax[:, bass.ds(t, 1)], accum_out=sums[:, bass.ds(t, 1)]).then_inc(expd, 1)
                    act.wait_ge(expd, t + 1)
                    act.wait_ge(pposed, t + 1)
                    nc.scalar.copy(ppair[:, par, 0, :], probs[:, par, :]).then_inc(phi_done, 1)

                def p_copy(t, par):
                    act.wait_ge(pposed, t + 3)
                    act.wait_ge(readout, t + 1)
                    nc.scalar.copy(pT[:, par, 0:TC, :], psP[:, 0, :, :]).then_inc(p_hi_copied, 1)

                def step(t, par, further_x, further_p):
                    p_copy(t, par)
                    if further_x > 1:
                        x_hi(t + 4, par)
                    if further_p:
                        exponentials(t + 1, 1 - par)
                    if further_x:
                        x_copy(t + 3, 1 - par)

                act.sem_inc(xcopied, 1)
                act.sem_inc(p_hi_copied, 1)
                x_hi(0, 0)
                x_hi(1, 1)
                x_copy(0, 0)
                x_hi(2, 0)
                x_copy(1, 1)
                x_hi(3, 1)
                exponentials(0, 0)
                x_copy(2, 0)
                with act.Fori(0, NT // 2 - 2) as i:
                    step(2 * i, 0, 2, True)
                    step(2 * i + 1, 1, 2, True)
                step(NT - 4, 0, 1, True)
                step(NT - 3, 1, 0, True)
                step(NT - 2, 0, 0, True)
                step(NT - 1, 1, 0, False)

            @block.vector
            def _(dve):
                def normalise(t):
                    if not (isinstance(t, int) and t == 0):
                        dve.wait_ge(xlo_done, t)
                    nc.vector.tensor_scalar(xn[:, :], xres[:, bass.ds(t, 1), :].rearrange("p o d -> p (o d)"),
                                            moments[:, bass.ds(t, 1), 0], rstd[:, bass.ds(t, 1)],
                                            ALU.subtract, ALU.mult).then_inc(normed, 1)

                def x_lo(t, par):
                    dve.wait_ge(xhi_done, t + 1)
                    nc.vector.tensor_tensor(xpair[:, par, 1, :], xn[:, :], xpair[:, par, 0, :],
                                            ALU.subtract).then_inc(xlo_done, 1)

                def mask_and_max(t, par, b):
                    dve.wait_ge(scored, t + 3)
                    if not (isinstance(t, int) and t < 2):
                        dve.wait_ge(plo_done, t - 1)
                    nc.vector.scalar_tensor_tensor(probs[:, par, :], psS[:, par, :], SC,
                                                   maskb[:, bass.ds(b, 1), :].rearrange("p o t -> p (o t)"),
                                                   ALU.mult, ALU.add).then_inc(masked, 1)
                    dve.wait_ge(masked, t + 3)
                    nc.vector.tensor_reduce(nmax[:, bass.ds(t, 1)], probs[:, par, :], AX_X, ALU.max,
                                            negate=True).then_inc(maxed, 1)

                def p_lo(t, par):
                    dve.wait_ge(phi_done, t + 1)
                    nc.vector.tensor_tensor(ppair[:, par, 1, :], probs[:, par, :], ppair[:, par, 0, :],
                                            ALU.subtract).then_inc(plo_done, 1)

                def p_copy(t, par):
                    dve.wait_ge(pposed, t + 3)
                    dve.wait_ge(readout, t + 1)
                    nc.vector.tensor_copy(pT[:, par, TC:2 * TC, :], psP[:, 1, :, :]).then_inc(p_lo_copied, 1)

                def update(t, b):
                    row = xres[:, bass.ds(t, 1), :].rearrange("p o d -> p (o d)")
                    nc.vector.reciprocal(rsum[:, bass.ds(t, 1)], sums[:, bass.ds(t, 1)]).then_inc(rsum_ready, 1)
                    dve.wait_ge(rsum_ready, t + 1)
                    nc.vector.tensor_tensor(coef[:, bass.ds(t, 1)], rsum[:, bass.ds(t, 1)], factor[:, bass.ds(b, 1)],
                                            ALU.mult).then_inc(coef_ready, 1)
                    dve.wait_ge(coef_ready, t + 1)
                    dve.wait_ge(readout, t + 3)
                    nc.vector.scalar_tensor_tensor(row, psR[:, :], coef[:, bass.ds(t, 1)], row,
                                                   ALU.mult, ALU.add).then_inc(updated, 1)
                    dve.wait_ge(updated, t + 2)
                    nc.vector.bn_stats(stats[:, bass.ds(t, 1), :].rearrange("p o d -> p (o d)"), row).then_inc(stats_ready, 1)

                def step(t, par, earlier, further_x, further_p):
                    p_copy(t, par)
                    if earlier:
                        update(t - 1, (t - 1) // QD)
                    if further_x:
                        normalise(t + 4)
                    if further_p:
                        mask_and_max(t + 1, 1 - par, (t + 1) // QD)
                    if further_x:
                        x_lo(t + 4, par)
                    if further_p:
                        p_lo(t + 1, 1 - par)

                for s, n in ((xposed, 2), (scored, 2), (masked, 2), (pposed, 2), (p_lo_copied, 1), (readout, 2), (updated, 1)):
                    dve.sem_inc(s, n)
                dve.wait_ge(rstd_ready, 3)
                for t in range(4):
                    normalise(t)
                    x_lo(t, t % 2)
                dve.wait_ge(mask_loaded, 16)
                nc.vector.tensor_scalar(maskb[:, :, :].rearrange("p b t -> p (b t)"),
                                        mask8[:, :, :].rearrange("p b t -> p (b t)"),
                                        1e30, -1e30, ALU.mult, ALU.add).then_inc(setup, 1)
                nc.vector.tensor_reduce(anyb[:, :], mask8[:, :, :], AX_X, ALU.max).then_inc(setup, 1)
                dve.wait_ge(setup, 2)
                nc.vector.tensor_scalar(factor[:, :], anyb[:, :], gates[:, 0:1], None, ALU.mult).then_inc(setup, 1)
                dve.wait_ge(setup, 3)
                mask_and_max(0, 0, 0)
                p_lo(0, 0)
                step(0, 0, False, True, True)
                step(1, 1, True, True, True)
                with dve.Fori(1, NT // 2 - 2) as i:
                    step(2 * i, 0, True, True, True)
                    step(2 * i + 1, 1, True, True, True)
                step(NT - 4, 0, True, False, True)
                step(NT - 3, 1, True, False, True)
                step(NT - 2, 0, True, False, True)
                step(NT - 1, 1, True, False, False)
                update(NT - 1, B - 1)
                dve.wait_ge(stats_ready, NT)
                for t in range(NT):
                    nc.vector.bn_aggr(moments[:, t, :], stats[:, t, :]).then_inc(moments_ready, 1)

            @block.tensor
            def _(pe):
                def x_transposes(t, par):
                    pe.wait_ge(xlo_done, t + 1)
                    pe.wait_ge(xcopied, t + 1)
                    for r in range(2):
                        for k in range(KC):
                            last = nc.tensor.transpose(psX[:, r * KC + k, :], xpair[:, par, r, k * P:(k + 1) * P], ident[:, :])
                    last.then_inc(xposed, 1)

                def scores(t, par, b):
                    pe.wait_ge(xcopied, t + 2)
                    pe.wait_ge(masked, t + 1)
                    for h in range(2):
                        n = 0
                        for ra, rb in ((0, 0), (0, 1), (1, 0)):
                            for k in range(KC):
                                last = nc.tensor.matmul(psS[:, par, h * 512:(h + 1) * 512], xT[:, par, ra * KC + k, :],
                                                        ctxT[:, rb * KC + k, bass.ds(b * T + h * 512, 512)],
                                                        start=(n == 0), stop=(n == 3 * KC - 1))
                                n += 1
                    last.then_inc(scored, 1)

                def p_transposes(t, par):
                    pe.wait_ge(plo_done, t + 1)
                    pe.wait_ge(p_hi_copied, t + 1)
                    pe.wait_ge(p_lo_copied, t + 1)
                    for r in range(2):
                        for k in range(TC):
                            last = nc.tensor.transpose(psP[:, r, k, :], ppair[:, par, r, k * P:(k + 1) * P], ident[:, :])
                    last.then_inc(pposed, 1)

                def read(t, par, b):
                    pe.wait_ge(p_hi_copied, t + 2)
                    pe.wait_ge(p_lo_copied, t + 2)
                    pe.wait_ge(updated, t + 1)
                    n = 0
                    for ra, rb in ((0, 0), (0, 1), (1, 0)):
                        for k in range(TC):
                            last = nc.tensor.matmul(psR[:, :], pT[:, par, ra * TC + k, :],
                                                    ctxN[:, bass.ds(b * TC + k, 1), rb, :].rearrange("p o d -> p (o d)"),
                                                    start=(n == 0), stop=(n == 3 * TC - 1))
                            n += 1
                    last.then_inc(readout, 1)

                def step(t, par, further_x, further_s):
                    p_transposes(t, par)
                    if further_s:
                        scores(t + 2, par, (t + 2) // QD)
                    if further_x:
                        x_transposes(t + 3, 1 - par)
                    read(t, par, t // QD)

                x_transposes(0, 0)
                x_transposes(1, 1)
                scores(0, 0, 0)
                x_transposes(2, 0)
                scores(1, 1, 0)
                with pe.Fori(0, NT // 2 - 2) as i:
                    step(2 * i, 0, True, True)
                    step(2 * i + 1, 1, True, True)
                step(NT - 4, 0, True, True)
                step(NT - 3, 1, False, True)
                step(NT - 2, 0, False, False)
                step(NT - 1, 1, False, False)


def router_phase(nc, sem, router_w, weights, ident, xres, moments, wT, scales, expert_of, place, dispatch_dram):
    NS = NT + E - 1
    with ExitStack() as c:
        sb = lambda name, shape, dt: c.enter_context(nc.sbuf_tensor(name, shape, dt))
        w32 = sb("r_w32", [P, 3, KC, D], F32)
        tern = sb("r_tern", [P, 3, KC, D], BF16)
        absum = sb("r_absum", [P, 3], F32)
        rmean = sb("r_rmean", [P, 3], F32)
        mean3 = sb("r_mean3", [P, 3], F32)
        means = sb("r_means", [P, E, 3], F32)
        onesf = sb("r_onesf", [P, P], F32)
        onesb = sb("r_onesb", [P, P], BF16)
        upper = sb("r_upper", [P, P], BF16)
        rT = sb("r_rT", [P, 2 * KC, E], BF16)
        half = sb("r_half", [P, NT], F32)
        veps = sb("r_veps", [P, NT], F32)
        rstd = sb("r_rstd", [P, NT], F32)
        xn = sb("r_xn", [P, 2, D], F32)
        q32 = sb("r_q32", [P, 2, D], F32)
        xpair = sb("r_xpair", [P, 2, 2, D], BF16)
        xT = sb("r_xT", [P, 2, 2 * KC, P], BF16)
        rows = q32[:, 0, :]
        rpair = xpair[:, 0, :, :]
        amax = sb("r_amax", [P, NT], F32)
        peak = sb("r_peak", [P, 2, 2], F32)
        invs = sb("r_invs", [P, 2], F32)
        disp = sb("r_disp", [P, NT, DW], BF16)
        logits = sb("r_logits", [P, NT, E], F32)
        psW = c.enter_context(nc.psum_tensor("r_psW", [P, 2, 2, KC, P], BF16))
        psX = c.enter_context(nc.psum_tensor("r_psX", [P, 2 * KC, P], BF16))
        psA = c.enter_context(nc.psum_tensor("r_psA", [P, 512], F32))
        psL = c.enter_context(nc.psum_tensor("r_psL", [P, 2, 256], F32))
        psC = c.enter_context(nc.psum_tensor("r_psC", [P, 2, 512], F32))
        zero_set, zero_stored = sem("r_zero_set"), sem("r_zero_stored")
        consts = sem("r_consts")
        router_loaded, router_hi, router_lo, router_xposed, router_ready = (
            sem("r_router_loaded"), sem("r_router_hi"), sem("r_router_lo"), sem("r_router_xposed"), sem("r_router_ready"))
        loaded = [sem(f"r_loaded{i}") for i in range(3)]
        abs_done, summed, mean_ready, rmean_ready = sem("r_abs_done"), sem("r_summed"), sem("r_mean_ready"), sem("r_rmean_ready")
        scaled, clamped, cast = sem("r_scaled"), sem("r_clamped"), sem("r_cast")
        w_xposed, w_even, w_odd = sem("r_w_xposed"), sem("r_w_even"), sem("r_w_odd")
        normed, amax_raw, amax_ready, invs_ready, q_ready = (
            sem("r_normed"), sem("r_amax_raw"), sem("r_amax_ready"), sem("r_invs_ready"), sem("r_q_ready"))
        q_cast, x_hi, x_lo, xposed, xcopied, judged, logits_ready = (
            sem("r_q_cast"), sem("r_x_hi"), sem("r_x_lo"), sem("r_xposed"), sem("r_xcopied"), sem("r_judged"), sem("r_logits_ready"))
        onehot_ready, counted, placed, scattered = sem("r_onehot_ready"), sem("r_counted"), sem("r_placed"), sem("r_scattered")
        chain, amax_kept, mean_kept = sem("r_chain"), sem("r_amax_kept"), sem("r_mean_kept")

        iota_e = sb("r_iota_e", [P, NS, E], F32)
        iota_j = sb("r_iota_j", [P, NS, E], F32)
        iota_c = sb("r_iota_c", [P, E, NT], F32)
        rank = sb("r_rank", [P, NT, E], F32)
        top = sb("r_top", [P, NT, 1], F32)
        key = sb("r_key", [P, NT, E], F32)
        onehot = sb("r_onehot", [P, NT, E], F32)
        onehotb = sb("r_onehotb", [P, NT, E], BF16)
        scan = [sb(f"r_scan{i}", [P, NT // 2 + NT, E], F32) for i in range(2)]
        counts = sb("r_counts", [P, E, 1], F32)
        tiles = sb("r_tiles", [P, E], F32)
        escan = [sb(f"r_escan{i}", [P, E // 2 + E], F32) for i in range(2)]
        start = sb("r_start", [P, 1, E], F32)
        placef = sb("r_placef", [P, NT], F32)
        owner = sb("r_owner", [P, NS, 1], F32)
        escale = sb("r_escale", [P, 2, 1, E], F32)
        carve = lambda u, n, k: w32[:, 0, u, 0:n * k].rearrange("p (n k) -> p n k", k=k)
        above, slot, ended, mine = carve(0, E, NT), carve(1, NT, E), carve(2, NS, E), carve(3, NS, E)
        picked = w32[:, 1, 0, 0:NS * E].rearrange("p (n k) -> p n k", k=E)

        with nc.Block() as block:
            @block.gpsimd
            def _(pool):
                steps = [0]

                def done(ins):
                    steps[0] += 1
                    ins.then_inc(consts, 1)
                    pool.wait_ge(consts, steps[0])

                nc.gpsimd.memset(wT[:, E - 2:E, :, :, :], 0.0).then_inc(zero_set, 1)
                pool.wait_ge(zero_set, 1)
                done(nc.gpsimd.memset(rows, 0.0))
                done(nc.gpsimd.memset(half[:, :], -0.5))
                done(nc.gpsimd.memset(onesf[:, :], 1.0))
                done(nc.gpsimd.memset(onesb[:, :], 1.0))
                done(nc.gpsimd.tensor_scalar(veps[:, :], moments[:, :, 1], EPS, None, ALU.add))
                done(nc.gpsimd.tensor_tensor(rstd[:, :], veps[:, :], half[:, :], ALU.pow))
                done(nc.gpsimd.affine_select(out=upper[:, :], in_=onesb[:, :], compare_op=ALU.is_ge, fill=0.0,
                                             base=0, pattern=[[1, P]], channel_multiplier=-1))
                imprecise = dict(channel_multiplier=0, allow_small_or_imprecise_dtypes=True)
                done(nc.gpsimd.iota(iota_e[:, :, :], [[0, NS], [1, E]], base=0, **imprecise))
                done(nc.gpsimd.iota(iota_j[:, :, :], [[1, NS], [0, E]], base=0, **imprecise))
                done(nc.gpsimd.iota(iota_c[:, :, :], [[0, E], [P, NT]], base=0, **imprecise))
                done(nc.gpsimd.iota(rank[:, :, :], [[0, NT], [-1, E]], base=E, **imprecise))
                for z in (scan[0][:, :, :], scan[1][:, :, :], escan[0][:, :], escan[1][:, :]):
                    done(nc.gpsimd.memset(z, 0.0))
                done(nc.gpsimd.memset(disp[:, :, D + 2:DW], 0.0))
                pool.wait_ge(placed, 2)
                pool.wait_ge(zero_stored, 16)
                pool.wait_ge(q_cast, NT + 2)
                for t in range(NT):
                    nc.gpsimd.indirect_dma_start(dispatch_dram[:, :], bass.IndirectOffsetOnAxis(place[:, t:t + 1], 0),
                                                 disp[:, t, :].bitcast(F32), None).then_inc(scattered, 16)
                pool.wait_ge(scattered, 16 * NT)

            CONSTS = 16

            @block.sync
            def _(sp):
                def load(e):
                    for m in range(3):
                        sp.wait_ge(cast, 3 * e + m + 1)
                        sp.dma_start(w32[:, m, :, :], weights[m][bass.ds(e, 1)].rearrange("o (u p) d -> p (o u) d", p=P)
                                     ).then_inc(loaded[m], 16)
                load(0)
                sp.wait_ge(consts, 1)
                sp.dma_start(rows[0:E, :], router_w).then_inc(router_loaded, 16)
                sp.wait_ge(zero_set, 1)
                sp.dma_start(dispatch_dram.rearrange("(p n) d -> p (n d)", p=P),
                             wT[:, E - 2:E, :, :, :].rearrange("p e m k d -> p (e m k d)")[:, 0:NS * DW].bitcast(F32)).then_inc(zero_stored, 16)
                with sp.Fori(1, E) as e:
                    load(e)

            @block.scalar
            def _(act):
                def expert(e):
                    for m in range(3):
                        act.wait_ge(loaded[m], e * 16 + 16)
                        act.wait_ge(summed, e + 1)
                        act.wait_ge(w_xposed, 3 * e + m + 1)
                        nc.scalar.activation(tern[:, m, :, :], w32[:, m, :, :], ACT.Abs,
                                             accum_out=absum[:, m:m + 1]).then_inc(abs_done, 1)
                    for j in range(2):
                        act.wait_ge(normed, 2 * e + j + 1)
                        act.wait_ge(xposed, 2 * e + j + 1)
                        nc.scalar.copy(xpair[:, j, 0, :], xn[:, j, :]).then_inc(x_hi, 1)
                    for j in range(2):
                        act.wait_ge(q_ready, 2 * e + j + 1)
                        nc.scalar.activation(disp[:, bass.ds(2 * e + j, 1), 0:D].rearrange("p o d -> p (o d)"), q32[:, j, :],
                                             ACT.Copy, bias=-MAGIC).then_inc(q_cast, 1)
                    for j in range(2):
                        act.wait_ge(xposed, 2 * e + j + 3)
                        act.wait_ge(judged, 2 * e + j + 1)
                        nc.scalar.copy(xT[:, j, :, :], psX[:, :, :]).then_inc(xcopied, 1)
                    for m in range(3):
                        act.wait_ge(clamped, 3 * e + m + 1)
                        act.wait_ge(w_xposed, 3 * e + m + 1)
                        nc.scalar.activation(tern[:, m, :, :], w32[:, m, :, :], ACT.Copy, bias=-MAGIC).then_inc(cast, 1)
                    act.wait_ge(zero_stored, 16)
                    for m in range(3):
                        act.wait_ge(w_xposed, 3 * e + m + 4)
                        for u in range(2):
                            last = nc.scalar.copy(wT[:, bass.ds(e, 1), m, :, u * P:(u + 1) * P].rearrange("p o k s -> p (o k) s"),
                                                  psW[:, 0, u, :, :])
                        last.then_inc(w_even, 1)

                for s, n in ((cast, 3), (q_cast, 2), (xcopied, 1), (w_even, 1)):
                    act.sem_inc(s, n)
                act.wait_ge(consts, 1)
                act.wait_ge(router_loaded, 16)
                nc.scalar.copy(rpair[:, 0, :], rows[:, :]).then_inc(router_hi, 1)
                act.wait_ge(router_xposed, 1)
                nc.scalar.copy(rT[:, :, :], psX[:, :, 0:E]).then_inc(router_ready, 1)
                with act.Fori(0, E) as e:
                    expert(e)

            @block.vector
            def _(dve):
                v = nc.vector

                def expert(e):
                    t = 2 * e
                    pair = lambda a: a[:, bass.ds(t, 2)]
                    for j in range(2):
                        dve.wait_ge(x_lo, t + j + 1)
                        v.tensor_scalar(xn[:, j, :], xres[:, bass.ds(t + j, 1), :].rearrange("p o d -> p (o d)"),
                                        moments[:, bass.ds(t + j, 1), 0], rstd[:, bass.ds(t + j, 1)],
                                        ALU.subtract, ALU.mult).then_inc(normed, 1)
                    dve.wait_ge(normed, t + 2)
                    v.tensor_reduce(peak[:, 0, :], xn[:, :, :], AX_X, ALU.max, apply_absolute_value=True).then_inc(amax_raw, 1)
                    dve.wait_ge(amax_raw, e + 1)
                    v.tensor_scalar(peak[:, 1, :], peak[:, 0, :], EPS, 1.0 / 127.0, ALU.max, ALU.mult).then_inc(amax_ready, 1)
                    dve.wait_ge(amax_ready, e + 1)
                    v.reciprocal(invs[:, :], peak[:, 1, :]).then_inc(invs_ready, 1)
                    v.tensor_copy(pair(amax), peak[:, 1, :]).then_inc(amax_kept, 1)
                    dve.wait_ge(amax_kept, e + 1)
                    dve.wait_ge(invs_ready, e + 1)
                    for j in range(2):
                        dve.wait_ge(q_cast, t + j + 1)
                        v.tensor_scalar(q32[:, j, :], xn[:, j, :], invs[:, j:j + 1], MAGIC, ALU.mult, ALU.add).then_inc(q_ready, 1)
                    for j in range(2):
                        dve.wait_ge(x_hi, t + j + 1)
                        v.tensor_tensor(xpair[:, j, 1, :], xn[:, j, :], xpair[:, j, 0, :], ALU.subtract).then_inc(x_lo, 1)
                    dve.wait_ge(summed, e + 2)
                    v.tensor_scalar(mean3[:, :], psA[:, 0:3], 1.0 / (D * D), EPS, ALU.mult, ALU.max).then_inc(mean_ready, 1)
                    dve.wait_ge(mean_ready, e + 2)
                    v.reciprocal(rmean[:, :], mean3[:, :]).then_inc(rmean_ready, 1)
                    v.tensor_copy(means[:, bass.ds(e, 1), :].rearrange("p o m -> p (o m)"), mean3[:, :]).then_inc(mean_kept, 1)
                    dve.wait_ge(mean_kept, e + 1)
                    dve.wait_ge(rmean_ready, e + 1)
                    for m in range(3):
                        v.tensor_scalar(w32[:, m, :, :], w32[:, m, :, :], rmean[:, m:m + 1], 1.0, ALU.mult, ALU.min).then_inc(scaled, 1)
                    for m in range(3):
                        dve.wait_ge(scaled, 3 * e + m + 1)
                        v.tensor_scalar(w32[:, m, :, :], w32[:, m, :, :], -1.0, MAGIC, ALU.max, ALU.add).then_inc(clamped, 1)
                    dve.wait_ge(judged, t + 4)
                    v.tensor_copy(logits[:, bass.ds(t, 2), :], psL[:, :, 0:E]).then_inc(logits_ready, 1)
                    dve.wait_ge(zero_stored, 16)
                    for m in range(3):
                        dve.wait_ge(w_xposed, 3 * e + m + 4)
                        for u in range(2):
                            last = v.tensor_copy(wT[:, bass.ds(e, 1), m, :, (2 + u) * P:(3 + u) * P].rearrange("p o k s -> p (o k) s"),
                                                 psW[:, 1, u, :, :])
                        last.then_inc(w_odd, 1)

                for s, n in ((summed, 1), (mean_ready, 1), (x_lo, 2), (w_xposed, 3), (w_odd, 1), (xposed, 2), (judged, 2),
                             (logits_ready, 1)):
                    dve.sem_inc(s, n)
                dve.wait_ge(consts, CONSTS)
                dve.wait_ge(router_hi, 1)
                v.tensor_tensor(rpair[:, 1, :], rows[:, :], rpair[:, 0, :], ALU.subtract).then_inc(router_lo, 1)
                with dve.Fori(0, E) as e:
                    expert(e)

                steps = [0]

                def then(ins):
                    steps[0] += 1
                    ins.then_inc(chain, 1)
                    dve.wait_ge(chain, steps[0])

                dve.wait_ge(logits_ready, E + 1)
                then(v.tensor_reduce(top[:, :, 0], logits[:, :, :], AX_X, ALU.max))
                then(v.tensor_tensor(key[:, :, :], logits[:, :, :], top[:, :, :].to_broadcast([P, NT, E]), ALU.is_equal))
                then(v.tensor_tensor(key[:, :, :], key[:, :, :], rank[:, :, :], ALU.mult))
                then(v.tensor_reduce(top[:, :, 0], key[:, :, :], AX_X, ALU.max))
                then(v.tensor_tensor(onehot[:, :, :], rank[:, :, :], top[:, :, :].to_broadcast([P, NT, E]), ALU.is_equal))
                v.tensor_copy(onehotb[:, :, :], onehot[:, :, :]).then_inc(onehot_ready, 1)
                Z = NT // 2
                dve.wait_ge(counted, 1)
                then(v.tensor_copy(scan[0][:, Z:, :], psC[:, 1, 0:P].rearrange("p (t e) -> p t e", e=E)))
                for i, d in enumerate((1, 2, 4, 8)):
                    a, b = scan[i % 2], scan[1 - i % 2]
                    then(v.tensor_tensor(b[:, Z:, :], a[:, Z:, :], a[:, Z - d:Z - d + NT, :], ALU.add))
                upto = scan[0]
                then(v.tensor_copy(counts[:, :, 0], upto[:, Z + NT - 1, :]))
                then(v.tensor_tensor(above[:, :, :], counts[:, :, :].to_broadcast([P, E, NT]), iota_c[:, :, :], ALU.is_gt))
                then(v.tensor_reduce(tiles[:, :], above[:, :, :], AX_X, ALU.add))
                H = E // 2
                then(v.tensor_copy(escan[0][:, H:], tiles[:, :]))
                for i, d in enumerate((1, 2, 4)):
                    a, b = escan[i % 2], escan[1 - i % 2]
                    then(v.tensor_tensor(b[:, H:], a[:, H:], a[:, H - d:H - d + E], ALU.add))
                ends = escan[1]
                then(v.tensor_tensor(start[:, 0, :], ends[:, H:], tiles[:, :], ALU.subtract))
                then(v.tensor_scalar(start[:, 0, :], start[:, 0, :], float(P), -1.0, ALU.mult, ALU.add))
                then(v.tensor_tensor(slot[:, :, :], upto[:, Z:, :], psC[:, 1, 0:P].rearrange("p (t e) -> p t e", e=E), ALU.subtract))
                then(v.tensor_tensor(slot[:, :, :], slot[:, :, :], start[:, :, :].to_broadcast([P, NT, E]), ALU.add))
                then(v.tensor_tensor(slot[:, :, :], slot[:, :, :], psC[:, 0, 0:P].rearrange("p (t e) -> p t e", e=E), ALU.add))
                then(v.tensor_tensor(slot[:, :, :], slot[:, :, :], onehot[:, :, :], ALU.mult))
                then(v.tensor_reduce(placef[:, :], slot[:, :, :], AX_X, ALU.add))
                v.tensor_copy(place[:, :], placef[:, :]).then_inc(placed, 1)
                then(v.tensor_tensor(top[:, :, 0], amax[:, :], amax[:, :], ALU.mult))
                v.tensor_tensor(disp[:, :, D:D + 2].bitcast(F32).rearrange("p t o -> p (t o)"), top[:, :, 0], amax[:, :],
                                ALU.mult).then_inc(placed, 1)
                then(v.tensor_tensor(ended[:, :, :], ends[:, H:].rearrange("p (o e) -> p o e", o=1).to_broadcast([P, NS, E]),
                                     iota_j[:, :, :], ALU.is_le))
                then(v.tensor_reduce(owner[:, :, 0], ended[:, :, :], AX_X, ALU.add))
                then(v.tensor_scalar(owner[:, :, 0], owner[:, :, 0], float(E - 1), None, ALU.min))
                then(v.tensor_copy(expert_of[:, :], owner[:, :, 0]))
                then(v.tensor_tensor(mine[:, :, :], iota_e[:, :, :], owner[:, :, :].to_broadcast([P, NS, E]), ALU.is_equal))
                then(v.tensor_tensor(escale[:, 0, 0, :], means[:, :, 0], means[:, :, 0], ALU.mult))
                then(v.tensor_tensor(escale[:, 0, 0, :], escale[:, 0, 0, :], means[:, :, 1], ALU.mult))
                then(v.tensor_copy(escale[:, 1, 0, :], means[:, :, 2]))
                for i in range(2):
                    then(v.tensor_tensor(picked[:, :, :], mine[:, :, :], escale[:, i, :, :].to_broadcast([P, NS, E]), ALU.mult))
                    then(v.tensor_reduce(scales[:, i, :], picked[:, :, :], AX_X, ALU.add))

            @block.tensor
            def _(pe):
                def expert(e):
                    pe.wait_ge(abs_done, 3 * e + 3)
                    pe.wait_ge(mean_ready, e + 1)
                    nc.tensor.matmul(psA[:, 0:3], onesf[:, :], absum[:, :], start=True, stop=True).then_inc(summed, 1)
                    for j in range(2):
                        t = 2 * e + j
                        pe.wait_ge(x_lo, t + 3)
                        pe.wait_ge(xcopied, t + 1)
                        for r in range(2):
                            for k in range(KC):
                                last = nc.tensor.transpose(psX[:, r * KC + k, :], xpair[:, j, r, k * P:(k + 1) * P], ident[:, :])
                        last.then_inc(xposed, 1)
                    pe.wait_ge(logits_ready, e + 1)
                    for j in range(2):
                        pe.wait_ge(xcopied, 2 * e + j + 2)
                        n = 0
                        for ra, rb in ((0, 0), (0, 1), (1, 0)):
                            for k in range(KC):
                                last = nc.tensor.matmul(psL[:, j, 0:E], xT[:, j, ra * KC + k, :], rT[:, rb * KC + k, :],
                                                        start=(n == 0), stop=(n == 3 * KC - 1))
                                n += 1
                        last.then_inc(judged, 1)
                    for m in range(3):
                        pe.wait_ge(cast, 3 * e + m + 4)
                        pe.wait_ge(w_even, 3 * e + m + 1)
                        pe.wait_ge(w_odd, 3 * e + m + 1)
                        for u in range(KC):
                            for k in range(KC):
                                last = nc.tensor.transpose(psW[:, u // 2, u % 2, k, :], tern[:, m, u, k * P:(k + 1) * P], ident[:, :])
                        last.then_inc(w_xposed, 1)

                pe.wait_ge(consts, CONSTS)
                pe.wait_ge(router_lo, 1)
                for r in range(2):
                    for k in range(KC):
                        last = nc.tensor.transpose(psX[:, r * KC + k, :], rpair[:, r, k * P:(k + 1) * P], ident[:, :])
                last.then_inc(router_xposed, 1)
                pe.wait_ge(router_ready, 1)
                with pe.Fori(0, E) as e:
                    expert(e)
                pe.wait_ge(onehot_ready, 1)
                cols = onehotb[:, :, :].rearrange("p t e -> p (t e)")
                nc.tensor.matmul(psC[:, 0, 0:P], upper[:, :], cols, start=True, stop=True)
                nc.tensor.matmul(psC[:, 1, 0:P], onesb[:, :], cols, start=True, stop=True).then_inc(counted, 1)


def mixture_phase(nc, sem, ident, wT, scales, expert_of, dispatch_dram, mixture_dram):
    NS = NT + E - 1
    with ExitStack() as c:
        sb = lambda name, shape, dt: c.enter_context(nc.sbuf_tensor(name, shape, dt))
        rows = sb("m_rows", [P, 4, DW], BF16)
        xT = sb("m_xT", [P, 2, KC, P], BF16)
        relu = sb("m_relu", [P, 2, D], F32)
        square = sb("m_square", [P, 2, D], F32)
        coef = sb("m_coef", [P, NS], F32)
        prod = sb("m_prod", [P, 2, D], F32)
        hmax = sb("m_hmax", [P, 2], F32)
        hinv = sb("m_hinv", [P, 2], F32)
        yscale = sb("m_yscale", [P, NS], F32)
        q32 = sb("m_q32", [P, 2, D], F32)
        hq = sb("m_hq", [P, 2, D], BF16)
        hT = sb("m_hT", [P, 2, KC, P], BF16)
        ys = sb("m_ys", [P, 2, D], F32)
        psG = c.enter_context(nc.psum_tensor("m_psG", [P, 2, 2, D], F32))
        psX = c.enter_context(nc.psum_tensor("m_psX", [P, 2 * KC, P], BF16))
        psH = c.enter_context(nc.psum_tensor("m_psH", [P, 2 * KC, P], BF16))
        psY = c.enter_context(nc.psum_tensor("m_psY", [P, 2, D], F32))
        loaded = [sem(f"m_loaded{i}") for i in range(4)]
        xposed = sem("m_xposed")
        xcopied, gated = sem("m_xcopied"), sem("m_gated")
        relu_done, squared, coef_ready, prod_ready = sem("m_relu_done"), sem("m_squared"), sem("m_coef_ready"), sem("m_prod_ready")
        hmax_raw, hmax_ready, hinv_ready, q_ready, q_cast = (
            sem("m_hmax_raw"), sem("m_hmax_ready"), sem("m_hinv_ready"), sem("m_q_ready"), sem("m_q_cast"))
        hposed, hcopied, lowered, yscale_ready, scaled = (
            sem("m_hposed"), sem("m_hcopied"), sem("m_lowered"), sem("m_yscale_ready"), sem("m_scaled"))
        stored = [sem(f"m_stored{i}") for i in range(2)]
        rows_v = dispatch_dram.rearrange("(n p) d -> n p d", p=P)
        out_v = mixture_dram.rearrange("(n p) d -> n p d", p=P)
        MAIN = (NS - 3) // 2 * 2
        assert NS - 3 == MAIN

        with nc.Block() as block:
            @block.sync
            def _(sp):
                def load(j, slot):
                    sp.wait_ge(xposed, j + 1)
                    sp.wait_ge(coef_ready, j + 1)
                    sp.dma_start(rows[:, slot, :].bitcast(F32), rows_v[bass.ds(j, 1)].rearrange("o p d -> p (o d)")).then_inc(loaded[slot], 16)

                def store(j, par):
                    sp.wait_ge(scaled, j + 3)
                    sp.dma_start(out_v[bass.ds(j, 1)].rearrange("o p d -> p (o d)"), ys[:, par, :]).then_inc(stored[par], 16)

                for i in range(2):
                    sp.sem_inc(stored[i], 16)
                for j in range(4):
                    load(j, j)
                with sp.Fori(0, (NS - 4) // 4) as i:
                    for k in range(4):
                        load(4 * i + k + 4, k)
                        store(4 * i + k, k % 2)
                for j in range((NS - 4) // 4 * 4, NS):
                    if j + 4 < NS:
                        load(j + 4, j % 4)
                    store(j, j % 2)
                for i in range(2):
                    sp.wait_ge(stored[i], 16 * (1 + (NS + 1 - i) // 2))

            @block.scalar
            def _(act):
                def x_copy(j, par):
                    act.wait_ge(xposed, j + 5)
                    act.wait_ge(gated, j + 1)
                    nc.scalar.copy(xT[:, par, :, :], psX[:, 0:KC, :]).then_inc(xcopied, 1)

                def squares(j, par):
                    act.wait_ge(gated, j + 3)
                    act.wait_ge(prod_ready, j + 1)
                    nc.scalar.activation(relu[:, par, :], psG[:, par, 0, :], ACT.Relu).then_inc(relu_done, 1)
                    act.wait_ge(relu_done, j + 1)
                    nc.scalar.activation(square[:, par, :], relu[:, par, :], ACT.Square).then_inc(squared, 1)

                def q_casts(j, par):
                    act.wait_ge(q_ready, j + 1)
                    act.wait_ge(hposed, j + 1)
                    nc.scalar.activation(hq[:, par, :], q32[:, par, :], ACT.Copy, bias=-MAGIC).then_inc(q_cast, 1)

                def h_copy(j, par):
                    act.wait_ge(hposed, j + 3)
                    act.wait_ge(lowered, j + 1)
                    nc.scalar.copy(hT[:, par, :, :], psH[:, 0:KC, :]).then_inc(hcopied, 1)

                def step(j, par, left):
                    h_copy(j, par)
                    if left >= 1:
                        q_casts(j + 1, 1 - par)
                    if left >= 2:
                        squares(j + 2, par)
                    if left >= 3:
                        x_copy(j + 3, 1 - par)

                for s, n in ((xcopied, 1), (hcopied, 1)):
                    act.sem_inc(s, n)
                x_copy(0, 0)
                x_copy(1, 1)
                squares(0, 0)
                x_copy(2, 0)
                squares(1, 1)
                q_casts(0, 0)
                with act.Fori(0, MAIN // 2) as i:
                    step(2 * i, 0, 3)
                    step(2 * i + 1, 1, 3)
                for j in range(MAIN, NS):
                    step(j, j % 2, NS - 1 - j)

            @block.vector
            def _(dve):
                v = nc.vector

                def coefficient(j, slot):
                    dve.wait_ge(loaded[slot], j // 4 * 16 + 16)
                    at = bass.ds(j, 1)
                    v.tensor_tensor(coef[:, at], rows[:, slot, D:D + 2].bitcast(F32), scales[:, 0, at], ALU.mult).then_inc(coef_ready, 1)

                def quantise(j, par):
                    at = bass.ds(j, 1)
                    dve.wait_ge(squared, j + 1)
                    dve.wait_ge(coef_ready, j + 5)
                    dve.wait_ge(q_ready, j) if not (isinstance(j, int) and j < 1) else None
                    v.scalar_tensor_tensor(prod[:, par, :], psG[:, par, 1, :], coef[:, at], square[:, par, :],
                                           ALU.mult, ALU.mult).then_inc(prod_ready, 1)
                    dve.wait_ge(prod_ready, j + 3)
                    v.tensor_reduce(hmax[:, par:par + 1], prod[:, par, :], AX_X, ALU.max, apply_absolute_value=True).then_inc(hmax_raw, 1)
                    dve.wait_ge(hmax_raw, j + 1)
                    v.tensor_scalar(hmax[:, par:par + 1], hmax[:, par:par + 1], EPS, 1.0 / 127.0, ALU.max, ALU.mult).then_inc(hmax_ready, 1)
                    dve.wait_ge(hmax_ready, j + 1)
                    v.reciprocal(hinv[:, par:par + 1], hmax[:, par:par + 1]).then_inc(hinv_ready, 1)
                    v.tensor_tensor(yscale[:, at], hmax[:, par:par + 1], scales[:, 1, at], ALU.mult).then_inc(yscale_ready, 1)
                    dve.wait_ge(yscale_ready, j + 1)
                    dve.wait_ge(hinv_ready, j + 1)
                    dve.wait_ge(q_cast, j + 1)
                    v.tensor_scalar(q32[:, par, :], prod[:, par, :], hinv[:, par:par + 1], MAGIC, ALU.mult, ALU.add).then_inc(q_ready, 1)

                def finish(j, par):
                    dve.wait_ge(lowered, j + 3)
                    dve.wait_ge(yscale_ready, j + 1)
                    dve.wait_ge(stored[par], j // 2 * 16 + 16)
                    v.tensor_scalar(ys[:, par, :], psY[:, par, :], yscale[:, bass.ds(j, 1)], None, ALU.mult).then_inc(scaled, 1)

                def step(j, par, left, coef_too, slot):
                    if left >= 2:
                        quantise(j + 2, par)
                    if coef_too:
                        coefficient(j + 4, slot)
                    finish(j, par)

                for s, n in ((xposed, 4), (coef_ready, 4), (gated, 2), (prod_ready, 2), (hposed, 2), (lowered, 2), (scaled, 2), (q_cast, 2)):
                    dve.sem_inc(s, n)
                for j in range(4):
                    coefficient(j, j)
                quantise(0, 0)
                quantise(1, 1)
                with dve.Fori(0, (NS - 4) // 4) as i:
                    for k in range(4):
                        step(4 * i + k, k % 2, 2, True, k)
                for j in range((NS - 4) // 4 * 4, NS):
                    step(j, j % 2, NS - 1 - j, j + 4 < NS, j % 4)

            @block.tensor
            def _(pe):
                def x_transposes(j, slot):
                    pe.wait_ge(loaded[slot], j // 4 * 16 + 16)
                    pe.wait_ge(xcopied, j + 1)
                    for k in range(KC):
                        last = nc.tensor.transpose(psX[:, k, :], rows[:, slot, k * P:(k + 1) * P], ident[:, :])
                    last.then_inc(xposed, 1)

                def weights_of(j):
                    e = nc.tensor.value_load(expert_of[0:1, bass.ds(j, 1)], min_val=0, max_val=E - 1)
                    return lambda m, k: wT[:, bass.ds(e, 1), m, k, :].rearrange("p o d -> p (o d)")

                def gate_and_up(j, par):
                    w = weights_of(j)
                    pe.wait_ge(xcopied, j + 2)
                    pe.wait_ge(prod_ready, j + 1)
                    for m in range(2):
                        for k in range(KC):
                            last = nc.tensor.matmul(psG[:, par, m, :], xT[:, par, k, :], w(m, k), start=(k == 0), stop=(k == KC - 1))
                    last.then_inc(gated, 1)

                def h_transposes(j, par):
                    pe.wait_ge(q_cast, j + 3)
                    pe.wait_ge(hcopied, j + 1)
                    for k in range(KC):
                        last = nc.tensor.transpose(psH[:, k, :], hq[:, par, k * P:(k + 1) * P], ident[:, :])
                    last.then_inc(hposed, 1)

                def down(j, par):
                    w = weights_of(j)
                    pe.wait_ge(hcopied, j + 2)
                    pe.wait_ge(scaled, j + 1)
                    for k in range(KC):
                        last = nc.tensor.matmul(psY[:, par, :], hT[:, par, k, :], w(2, k), start=(k == 0), stop=(k == KC - 1))
                    last.then_inc(lowered, 1)

                def step(j, par, left, slot3):
                    h_transposes(j, par)
                    if left >= 2:
                        gate_and_up(j + 2, par)
                    if left >= 3:
                        x_transposes(j + 3, slot3)
                    down(j, par)

                x_transposes(0, 0)
                x_transposes(1, 1)
                gate_and_up(0, 0)
                x_transposes(2, 2)
                gate_and_up(1, 1)
                with pe.Fori(0, (NS - 4) // 4) as i:
                    for k in range(4):
                        step(4 * i + k, k % 2, 3, (k + 3) % 4)
                for j in range((NS - 4) // 4 * 4, NS):
                    step(j, j % 2, NS - 1 - j, (j + 3) % 4)


def gather_phase(nc, sem, place, gates, mixture_dram, xres, moments):
    with ExitStack() as c:
        sb = lambda name, shape, dt: c.enter_context(nc.sbuf_tensor(name, shape, dt))
        rows = sb("g_rows", [P, NT, D], F32)
        stats = sb("g_stats", [P, NT, 6], F32)
        fetched = [sem(f"g_fetched{i}") for i in range(NT)]
        updated, stats_ready, moments_ready = sem("g_updated"), sem("g_stats_ready"), sem("g_moments_ready")
        with nc.Block() as block:
            @block.gpsimd
            def _(pool):
                for t in range(NT):
                    nc.gpsimd.indirect_dma_start(rows[:, t, :], None, mixture_dram[:, :],
                                                 bass.IndirectOffsetOnAxis(place[:, t:t + 1], 0)).then_inc(fetched[t], 16)

            @block.vector
            def _(dve):
                for t in range(NT):
                    dve.wait_ge(fetched[t], 16)
                    nc.vector.scalar_tensor_tensor(xres[:, t, :], rows[:, t, :], gates[:, 2:3], xres[:, t, :],
                                                   ALU.mult, ALU.add).then_inc(updated, 1)
                    dve.wait_ge(updated, t + 1)
                    nc.vector.bn_stats(stats[:, t, :], xres[:, t, :]).then_inc(stats_ready, 1)
                dve.wait_ge(stats_ready, NT)
                for t in range(NT):
                    nc.vector.bn_aggr(moments[:, t, :], stats[:, t, :]).then_inc(moments_ready, 1)


def query_phase(nc, wq, bq, wo, queries_dram, ident, xres, moments, woT):
    queries_v = queries_dram.rearrange("b r (c p) s -> b c p r s", p=P)
    NTILE = 2 * QD + NT
    with ExitStack() as c:
        sb = lambda name, shape, dt: c.enter_context(nc.sbuf_tensor(name, shape, dt))
        sem = lambda name: c.enter_context(nc.semaphore(name))
        w32 = sb("q_w32", [P, 2, QD, D], F32)
        bias = sb("q_bias", [P, KC], F32)
        wqT = sb("q_wqT", [P, 2 * KC, D], BF16)
        half = sb("q_half", [P, NT], F32)
        veps = sb("q_veps", [P, NT], F32)
        rstd = sb("q_rstd", [P, NT], F32)
        xn = sb("q_xn", [P, 4, D], F32)
        pair = sb("q_pair", [P, 4, 2, D], BF16)
        xT = sb("q_xT", [P, 2, 2 * KC, S], BF16)
        qst = sb("q_qst", [P, 4, 2, S], BF16)
        psX = c.enter_context(nc.psum_tensor("q_psX", [P, 2, 2 * KC, P], BF16))
        psG = c.enter_context(nc.psum_tensor("q_psG", [P, 4, 512], F32))
        w_loaded = [sem(f"q_w_loaded{i}") for i in range(2)]
        bias_loaded = sem("q_bias_loaded")
        rstd_ready = sem("q_rstd_ready")
        normed = sem("q_normed")
        hi_done, lo_done = sem("q_hi_done"), sem("q_lo_done")
        xposed = sem("q_xposed")
        even_copied, odd_copied = sem("q_even_copied"), sem("q_odd_copied")
        gemm_done = sem("q_gemm_done")
        hi_out, lo_out = sem("q_hi_out"), sem("q_lo_out")
        stored = [sem(f"q_stored{i}") for i in range(4)]

        def source(n):
            return w32[:, n // QD, n % QD, :] if n < 2 * QD else xn[:, n % 4, :]

        def target(n):
            if n < 2 * QD:
                return (wqT, woT)[n // QD][:, :, n % QD * P:(n % QD + 1) * P]
            t = n - 2 * QD
            return xT[:, t // QD % 2, :, t % QD * P:(t % QD + 1) * P]

        with nc.Block() as block:
            @block.gpsimd
            def _(pool):
                nc.gpsimd.memset(half[:, :], -0.5).then_inc(rstd_ready, 1)
                nc.gpsimd.tensor_scalar(veps[:, :], moments[:, :, 1], EPS, None, ALU.add).then_inc(rstd_ready, 1)
                pool.wait_ge(rstd_ready, 2)
                nc.gpsimd.tensor_tensor(rstd[:, :], veps[:, :], half[:, :], ALU.pow).then_inc(rstd_ready, 1)

            @block.sync
            def _(sp):
                for i, w in enumerate((wq, wo)):
                    sp.dma_start(w32[:, i, :, :], w.rearrange("(u p) d -> p u d", p=P)).then_inc(w_loaded[i], 16)
                sp.dma_start(bias[:, :], bq.rearrange("(c p) -> p c", p=P),
                             allow_slow_non_contiguous=True).then_inc(bias_loaded, 16)
                for b in range(B):
                    for k in range(KC):
                        sp.wait_ge(lo_out, b * KC + k + 1)
                        sp.dma_start(queries_v[b, k], qst[:, k, :, :]).then_inc(stored[k], 16)
                for k in range(KC):
                    sp.wait_ge(stored[k], 16 * B)

            @block.scalar
            def _(act):
                def split(n):
                    if n < 2 * QD:
                        act.wait_ge(w_loaded[n // QD], 16)
                    else:
                        act.wait_ge(normed, n - 2 * QD + 1)
                    if n >= 4:
                        act.wait_ge(xposed, n - 3)
                    nc.scalar.copy(pair[:, n % 4, 0, :], source(n)).then_inc(hi_done, 1)

                def copy(n):
                    act.wait_ge(xposed, n + 1)
                    if n >= 4 * QD:
                        act.wait_ge(gemm_done, ((n - 2 * QD) // QD - 1) * KC)
                    nc.scalar.copy(target(n), psX[:, 0, :, :]).then_inc(even_copied, 1)

                def evacuate(b):
                    for k in range(KC):
                        act.wait_ge(gemm_done, b * KC + k + 1)
                        if b > 0:
                            act.wait_ge(stored[k], 16 * b)
                        nc.scalar.activation(qst[:, k, 0, :], psG[:, k, :], ACT.Identity,
                                             bias=bias[:, k:k + 1]).then_inc(hi_out, 1)

                act.wait_ge(bias_loaded, 16)
                for n in range(NTILE):
                    split(n)
                    if n >= 2 and n % 2 == 0:
                        copy(n - 2)
                    if n >= 4 * QD - 1 and n % QD == 3:
                        evacuate((n - 4 * QD + 1) // QD)
                copy(NTILE - 2)
                evacuate(B - 1)

            @block.vector
            def _(dve):
                def normalise(t):
                    if t >= 4:
                        dve.wait_ge(lo_done, t + 2 * QD - 3)
                    nc.vector.tensor_scalar(xn[:, t % 4, :], xres[:, t, :], moments[:, t, 0:1], rstd[:, t:t + 1],
                                            ALU.subtract, ALU.mult).then_inc(normed, 1)

                def split(n):
                    dve.wait_ge(hi_done, n + 1)
                    nc.vector.tensor_tensor(pair[:, n % 4, 1, :], source(n), pair[:, n % 4, 0, :],
                                            ALU.subtract).then_inc(lo_done, 1)

                def copy(n):
                    dve.wait_ge(xposed, n + 1)
                    if n >= 4 * QD:
                        dve.wait_ge(gemm_done, ((n - 2 * QD) // QD - 1) * KC)
                    nc.vector.tensor_copy(target(n), psX[:, 1, :, :]).then_inc(odd_copied, 1)

                def evacuate(b):
                    for k in range(KC):
                        dve.wait_ge(hi_out, b * KC + k + 1)
                        nc.vector.scalar_tensor_tensor(qst[:, k, 1, :], psG[:, k, :], bias[:, k:k + 1],
                                                       qst[:, k, 0, :], ALU.add, ALU.subtract).then_inc(lo_out, 1)

                dve.wait_ge(bias_loaded, 16)
                for n in range(NTILE):
                    split(n)
                    if n == 2:
                        dve.wait_ge(rstd_ready, 3)
                    if n >= 2 and n + 2 < NTILE and n - 6 + 2 * QD < NTILE and n - 2 < 4:
                        normalise(n - 2)
                    if n >= 2 * QD and n - 4 < NT:
                        normalise(n - 4)
                    if n >= 2 and n % 2 == 1:
                        copy(n - 2)
                    if n >= 4 * QD - 1 and n % QD == 3:
                        evacuate((n - 4 * QD + 1) // QD)
                copy(NTILE - 1)
                evacuate(B - 1)

            @block.tensor
            def _(pe):
                def transposes(n):
                    pe.wait_ge(lo_done, n + 1)
                    if n >= 2:
                        pe.wait_ge((even_copied, odd_copied)[n % 2], n // 2)
                    for r in range(2):
                        for k in range(KC):
                            last = nc.tensor.transpose(psX[:, n % 2, r * KC + k, :], pair[:, n % 4, r, k * P:(k + 1) * P],
                                                       ident[:, :])
                    last.then_inc(xposed, 1)

                def gemm(b):
                    pe.wait_ge(even_copied, 2 * b + 6)
                    pe.wait_ge(odd_copied, 2 * b + 6)
                    for m in range(KC):
                        if b > 0:
                            pe.wait_ge(lo_out, (b - 1) * KC + m + 1)
                        n = 0
                        for ra, rb in ((0, 0), (0, 1), (1, 0)):
                            for k in range(KC):
                                last = nc.tensor.matmul(psG[:, m, :], wqT[:, ra * KC + k, m * P:(m + 1) * P],
                                                        xT[:, b % 2, rb * KC + k, :], start=(n == 0), stop=(n == 3 * KC - 1))
                                n += 1
                        last.then_inc(gemm_done, 1)

                for n in range(NTILE):
                    transposes(n)
                    if n >= 4 * QD - 1 and n % QD == 3:
                        gemm((n - 4 * QD + 1) // QD)
                gemm(B - 1)


def attention_phase(nc, queries_dram, keys_dram, values_dram, mixed_dram, ident):
    SC = float(HD) ** -0.5
    KR, AR = 3 * HD, 3 * HD + 3
    G = 4
    TC = T // P
    AHEAD, MAXAHEAD = 4, 6
    ER, PR = 4, 8
    HI_ON_DVE = (0,)
    LO_ON_POOL = (0, 2, 3)
    NLD = 10
    q_v = queries_dram.rearrange("b r (g h d) s -> b g r d h s", g=G, h=G)
    k_v = keys_dram.rearrange("(b n) r (g h d) t -> b g n r d h t", n=2, g=G, h=G)
    v_v = values_dram.rearrange("b (c p) (g n) -> b g p c n", p=P, g=G)
    mixed_v = mixed_dram.rearrange("b r (h d) s -> b h r d s", h=NH)

    with ExitStack() as c:
        sb = lambda name, shape, dt: c.enter_context(nc.sbuf_tensor(name, shape, dt))
        sem = lambda name: c.enter_context(nc.semaphore(name))
        qst = sb("t_qst", [AR, G, G, S], BF16)
        kst = sb("t_kst", [AR, G, G, T], BF16)
        vst = sb("t_vst", [P, G, TC, G, VW], BF16)
        e32 = sb("t_e32", [P, ER, 2, S], F32)
        probs = sb("t_probs", [P, PR, 2, 2, S], BF16)
        nmax = sb("t_nmax", [P, 2, G, 4], F32)
        nrest = sb("t_nrest", [P, G, 4], F32)
        nparts = sb("t_nparts", [P, P // (4 * G), G, 4], BF16)
        nrows = sb("t_nrows", [3 * 4 * G, P], BF16)
        ost = sb("t_ost", [VW, 2, S], F32)
        psM = c.enter_context(nc.psum_tensor("t_psM", [P, 2, 512], F32))
        psE = c.enter_context(nc.psum_tensor("t_psE", [P, 2, 2, S], F32))
        psO = c.enter_context(nc.psum_tensor("t_psO", [P, 2, S], F32))
        psN = psM[:, 0, 0:P // 2].bitcast(BF16)
        loaded = [sem(f"t_loaded{i}") for i in range(G)]
        max_loaded = [sem(f"t_max_loaded{i}") for i in range(G)]
        zeros_set, ones_set = sem("t_zeros_set"), sem("t_ones_set")
        max_scored, maxed = sem("t_max_scored"), sem("t_maxed")
        n1_done, nrest_done, n2_done, n3_done = (sem("t_n1_done"), sem("t_nrest_done"), sem("t_n2_done"), sem("t_n3_done"))
        n_xposed, n_copied = sem("t_n_xposed"), sem("t_n_copied")
        scored, expd = sem("t_scored"), sem("t_expd")
        hi_act, hi_dve = sem("t_hi_act"), sem("t_hi_dve")
        lo_dve, lo_pool = sem("t_lo_dve"), sem("t_lo_pool")
        mixed = sem("t_mixed")
        copied_out = sem("t_copied_out")
        stored = [sem(f"t_stored{i}") for i in range(2)]

        def upto(quarters, head, u):
            return head * len(quarters) + sum(q <= u for q in quarters)

        HI_ON_ACT = tuple(u for u in range(4) if u not in HI_ON_DVE)
        LO_ON_DVE = tuple(u for u in range(4) if u not in LO_ON_POOL)

        def wait_hi(eng, head, u):
            dve = u in HI_ON_DVE
            eng.wait_ge(hi_dve if dve else hi_act, upto(HI_ON_DVE if dve else HI_ON_ACT, head, u))

        def wait_lo(eng, head, u):
            pool = u in LO_ON_POOL
            eng.wait_ge(lo_pool if pool else lo_dve, upto(LO_ON_POOL if pool else LO_ON_DVE, head, u))

        def slot(h, u):
            return (h * 4 + u) % PR

        def ahead(b, h, u, n):
            h, u = h + (u + n) // 4, (u + n) % 4
            return b + h // NH, h % NH, u

        def steps(b):
            return [(b, h, u) for h in range(NH) for u in range(4)]

        LAST = B - 1
        EARLY = [(0, h, u) for h in range(MAXAHEAD) for u in range(4)]

        def within(b, h):
            return not (isinstance(b, int) and b > LAST)

        def max_group_ends(h, u):
            return h % G == G - 1 and u == 3

        with nc.Block() as block:
            @block.sync
            def _(sp):
                def load(b, g):
                    bb = bass.ds(b, 1)
                    def put(dst, src):
                        sp.dma_start(dst, src).then_inc(loaded[g], 16)
                    for i, r in enumerate((0, 1, 0)):
                        put(qst[i * HD:(i + 1) * HD, g, :, :], q_v[bb, g, r].rearrange("o d h s -> d (o h) s"))
                    for i, r in enumerate((0, 0, 1)):
                        for n in range(2):
                            put(kst[i * HD:(i + 1) * HD, g, :, n * 512:(n + 1) * 512],
                                k_v[bb, g, n, r].rearrange("o d h t -> d (o h) t"))
                    put(vst[:, g, :, :, :].rearrange("p c h w -> p c (h w)"),
                        v_v[bb, g].rearrange("o p c n -> p (o c) n"))

                def put_max(b, g):
                    sp.wait_ge(n_copied, b * G + g + 1)
                    sp.dma_start(qst[KR:AR, g, :, :].rearrange("r h (u s) -> r (h u) s", u=4),
                                 nrows[:, :]).then_inc(max_loaded[g], 16)

                def batch(b):
                    for h in range(NH):
                        if (h + 1) % G == 2:
                            b2, h2, _ = ahead(b, h + 1, 0, 4 * (MAXAHEAD - 1))
                            if within(b2, h2):
                                put_max(b2, h2 // G)
                        sp.wait_ge(copied_out, b * NH + h + 3)
                        sp.dma_start(mixed_v[bass.ds(b, 1), h].rearrange("o r d s -> (o r) d s"),
                                     ost[:, h % 2, :]).then_inc(stored[h % 2], 16)
                        if h % G == G - 1 and not (isinstance(b, int) and b == LAST):
                            sp.wait_ge(mixed, (b * NH + h) * 4 + 4 + PR)
                            load(b + 1, h // G)

                for i in range(2):
                    sp.sem_inc(stored[i], 16)
                for g in range(G):
                    load(0, g)
                put_max(0, 0)
                with sp.Fori(0, LAST) as b:
                    batch(b)
                batch(LAST)
                for i in range(2):
                    sp.wait_ge(stored[i], 16 * (B * NH // 2 + 1))

            @block.gpsimd
            def _(pool):
                def halves(b, h, u):
                    head = b * NH + h
                    if u in LO_ON_POOL:
                        wait_hi(pool, head, u)
                        pool.wait_ge(expd, head * 4 + u + 1)
                        nc.gpsimd.tensor_tensor(probs[:, slot(h, u), 1, :, :], e32[:, (h * 4 + u) % ER, :, :], probs[:, slot(h, u), 0, :, :],
                                                ALU.subtract).then_inc(lo_pool, 1)

                nc.gpsimd.memset(nparts[:, :, :, :], 0.0).then_inc(zeros_set, 1)
                pool.wait_ge(zeros_set, 1)
                nc.gpsimd.memset(kst[KR:AR, :, :, :], 1.0).then_inc(ones_set, 1)
                for n in range(AHEAD):
                    halves(*ahead(0, 0, 0, n))
                def batch(b):
                    for _, h, u in steps(b):
                        b2, h2, u2 = ahead(b, h, u, AHEAD)
                        if within(b2, h2):
                            halves(b2, h2, u2)
                with pool.Fori(0, LAST) as b:
                    batch(b)
                batch(LAST)

            @block.scalar
            def _(act):
                def exponentials(b, h, u):
                    head = b * NH + h
                    act.wait_ge(scored, head * 4 + u + 1)
                    if not (isinstance(b, int) and b == 0 and h * 4 + u < ER):
                        wait_lo(act, head + (u - ER) // 4, (u - ER) % 4)
                    if u in HI_ON_DVE:
                        nc.scalar.activation(e32[:, (h * 4 + u) % ER, :, :], psE[:, u % 2, :, :], ACT.Exp, scale=SC).then_inc(expd, 1)
                    else:
                        act.wait_ge(mixed, head * 4 + u + 1)
                        nc.scalar.activation(probs[:, slot(h, u), 0, :, :], psE[:, u % 2, :, :], ACT.Exp, scale=SC).then_inc(hi_act, 1)
                        nc.scalar.activation(e32[:, (h * 4 + u) % ER, :, :], psE[:, u % 2, :, :], ACT.Exp, scale=SC).then_inc(expd, 1)

                def copy_out(b, h):
                    head = b * NH + h
                    act.wait_ge(mixed, head * 4 + 4 + PR)
                    act.wait_ge(stored[h % 2], b * 16 * (NH // 2) + h // 2 * 16 + 16)
                    nc.scalar.copy(ost[:, h % 2, :], psO[0:VW, h % 2, :]).then_inc(copied_out, 1)

                act.sem_inc(copied_out, 2)
                act.sem_inc(mixed, PR)
                for n in range(AHEAD):
                    exponentials(*ahead(0, 0, 0, n))
                def batch(b):
                    for _, h, u in steps(b):
                        b2, h2, u2 = ahead(b, h, u, AHEAD)
                        if within(b2, h2):
                            exponentials(b2, h2, u2)
                        if u == 3:
                            copy_out(b, h)
                with act.Fori(0, LAST) as b:
                    batch(b)
                batch(LAST)

            @block.vector
            def _(dve):
                def maximum(b, h, u):
                    n = (b * NH + h) * 4 + u
                    dve.wait_ge(max_scored, n + 1)
                    nc.vector.tensor_reduce(nmax[:, h // G % 2, h % G, u:u + 1], psM[:, :, :].rearrange("p a t -> p (a t)"),
                                            AX_X, ALU.max, negate=True).then_inc(maxed, 1)

                def max_parts(b, g):
                    k = b * G + g
                    dve.wait_ge(maxed, k * 16 + 16)
                    m = nmax[:, g % 2, :, :]
                    if not (isinstance(b, int) and b == 0 and g == 0):
                        dve.wait_ge(n_xposed, k)
                    nc.vector.tensor_copy(nparts[:, 0, :, :], m).then_inc(n1_done, 1)
                    dve.wait_ge(n1_done, k + 1)
                    nc.vector.tensor_tensor(nrest[:, :, :], m, nparts[:, 0, :, :], ALU.subtract).then_inc(nrest_done, 1)
                    dve.wait_ge(nrest_done, k + 1)
                    nc.vector.tensor_copy(nparts[:, 1, :, :], nrest[:, :, :]).then_inc(n2_done, 1)
                    dve.wait_ge(n2_done, k + 1)
                    nc.vector.tensor_tensor(nparts[:, 2, :, :], nrest[:, :, :], nparts[:, 1, :, :],
                                            ALU.subtract).then_inc(n3_done, 1)

                def max_copy(b, g):
                    k = b * G + g
                    dve.wait_ge(n_xposed, k + 1)
                    if not (isinstance(b, int) and b == 0 and g == 0):
                        pb, pg = (b, g - 1) if g else (b - 1, G - 1)
                        dve.wait_ge(max_loaded[pg], pb * 16 + 16)
                    nc.vector.tensor_copy(nrows[:, :], psN[0:3 * G * 4, :]).then_inc(n_copied, 1)

                def low(b, h, u):
                    head = b * NH + h
                    if u in HI_ON_DVE:
                        dve.wait_ge(expd, head * 4 + u + 1)
                        dve.wait_ge(mixed, head * 4 + u + 1)
                        nc.vector.tensor_copy(probs[:, slot(h, u), 0, :, :], e32[:, (h * 4 + u) % ER, :, :]).then_inc(hi_dve, 1)
                    if u in LO_ON_DVE:
                        wait_hi(dve, head, u)
                        dve.wait_ge(expd, head * 4 + u + 1)
                        nc.vector.tensor_tensor(probs[:, slot(h, u), 1, :, :], e32[:, (h * 4 + u) % ER, :, :], probs[:, slot(h, u), 0, :, :],
                                                ALU.subtract).then_inc(lo_dve, 1)

                dve.wait_ge(zeros_set, 1)
                for b, h, u in EARLY:
                    maximum(b, h, u)
                    if max_group_ends(h, u):
                        max_parts(b, h // G)
                        max_copy(b, h // G)
                for n in range(AHEAD - 1):
                    low(*ahead(0, 0, 0, n))
                def batch(b):
                    for _, h, u in steps(b):
                        b2, h2, u2 = ahead(b, h, u, AHEAD - 1)
                        if within(b2, h2):
                            low(b2, h2, u2)
                        if h % G == 2 and u in (0, 2):
                            b3, h3, _ = ahead(b, h, 0, 4 * (MAXAHEAD - 1))
                            if within(b3, h3):
                                (max_parts if u == 0 else max_copy)(b3, h3 // G)
                        b2, h2, u2 = ahead(b, h, u, 4 * MAXAHEAD)
                        if within(b2, h2):
                            maximum(b2, h2, u2)
                with dve.Fori(0, LAST) as b:
                    batch(b)
                batch(LAST)

            @block.tensor
            def _(pe):
                def max_scores(b, h, u):
                    n = (b * NH + h) * 4 + u
                    g = h // G
                    if h % G == 0 and u == 0:
                        pe.wait_ge(loaded[g], b * 16 * NLD + 16 * NLD)
                    if not (isinstance(b, int) and b == 0 and h == 0 and u == 0):
                        pe.wait_ge(maxed, n)
                    for i in range(2):
                        last = nc.tensor.matmul(psM[:, i, :], qst[0:KR, g, h % G, u * P:(u + 1) * P],
                                                kst[0:KR, g, h % G, i * 512:(i + 1) * 512], start=True, stop=True)
                    last.then_inc(max_scored, 1)

                def max_transpose(b, g, seen):
                    k = b * G + g
                    pe.wait_ge(n3_done, k + 1)
                    pe.wait_ge(maxed, seen)
                    nc.tensor.transpose(psN, nparts[:, :, :, :].rearrange("p r h u -> p (r h u)"),
                                        ident[:, :]).then_inc(n_xposed, 1)

                def scores(b, h, u):
                    s = (b * NH + h) * 4 + u
                    g = h // G
                    if h % G == 0 and u == 0:
                        pe.wait_ge(max_loaded[g], b * 16 + 16)
                    if not (isinstance(b, int) and b == 0 and h == 0 and u < 2):
                        pe.wait_ge(expd, s - 1)
                    for i in range(2):
                        k = 2 * u + i
                        last = nc.tensor.matmul(psE[:, u % 2, i, :], kst[:, g, h % G, k * P:(k + 1) * P],
                                                qst[:, g, h % G, :], start=True, stop=True)
                    last.then_inc(scored, 1)

                def mix(b, h, u):
                    head = b * NH + h
                    g = h // G
                    wait_lo(pe, head, u)
                    if u == 0:
                        pe.wait_ge(copied_out, head + 1)
                    for i in range(2):
                        for r in range(2):
                            last = nc.tensor.matmul(psO[0:VW, h % 2, :], vst[:, g, 2 * u + i, h % G, :],
                                                    probs[:, slot(h, u), r, i, :], start=(u == 0 and i == 0 and r == 0),
                                                    stop=(u == 3 and i == 1 and r == 1))
                    last.then_inc(mixed, 1)

                pe.wait_ge(ones_set, 1)
                for b, h, u in EARLY:
                    max_scores(b, h, u)
                    if max_group_ends(h, u):
                        max_transpose(b, h // G, h * 4 + u + 1)
                        pe.wait_ge(n_copied, b * G + h // G + 1)
                for n in range(AHEAD):
                    scores(*ahead(0, 0, 0, n))
                def batch(b):
                    for _, h, u in steps(b):
                        if h % G == 2 and u == 2:
                            b3, h3, _ = ahead(b, h, 0, 4 * (MAXAHEAD - 1))
                            if within(b3, h3):
                                seen = (b * NH + h + MAXAHEAD) * 4 + u
                                max_transpose(b3, h3 // G, min(seen, B * NH * 4) if isinstance(b, int) else seen)
                        b2, h2, u2 = ahead(b, h, u, AHEAD)
                        if within(b2, h2):
                            scores(b2, h2, u2)
                        mix(b, h, u)
                        if h % G == 2 and u == 2 and within(b3, h3):
                            pe.wait_ge(n_copied, b3 * G + h3 // G + 1)
                        b2, h2, u2 = ahead(b, h, u, 4 * MAXAHEAD)
                        if within(b2, h2):
                            max_scores(b2, h2, u2)
                with pe.Fori(0, LAST) as b:
                    batch(b)
                batch(LAST)


def output_phase(nc, mixed_dram, bv, bo, ident, xres, woT, x3_dram, gates, xeT):
    PER = S // E
    parts_v = mixed_dram.rearrange("b r (c p) s -> b r p c s", p=P)
    xe_v = xeT[:, :, :, :].rearrange("p r (f e) (b s) -> p f b r e s", e=P // PER, b=B)
    with ExitStack() as c:
        sb = lambda name, shape, dt: c.enter_context(nc.sbuf_tensor(name, shape, dt))
        sem = lambda name: c.enter_context(nc.semaphore(name))
        parts = sb("o_parts", [P, 2, 3, KC, S], F32)
        bias = sb("o_bias", [P, KC], F32)
        bob = sb("o_bob", [P, D], F32)
        cpair = sb("o_cpair", [P, 2, 2, KC, S], BF16)
        half = sb("o_half", [P, NT], F32)
        stats = sb("o_stats", [P, NT, 6], F32)
        mom = sb("o_mom", [P, NT, 2], F32)
        veps = sb("o_veps", [P, NT], F32)
        rstd = sb("o_rstd", [P, NT], F32)
        xn = sb("o_xn", [P, 4, D], F32)
        xpair = sb("o_xpair", [P, 4, 2, D], BF16)
        psG = c.enter_context(nc.psum_tensor("o_psG", [P, 4, D], F32))
        psX = c.enter_context(nc.psum_tensor("o_psX", [P, 2, 2 * KC, P], BF16))
        consts_loaded = sem("o_consts_loaded")
        parts_loaded = [sem(f"o_parts_loaded{i}") for i in range(2)]
        half_set = sem("o_half_set")
        bo_gated, biased = sem("o_bo_gated"), sem("o_biased")
        rsum_ready, summed, divided = sem("o_rsum_ready"), sem("o_summed"), sem("o_divided")
        c_hi, c_lo = sem("o_c_hi"), sem("o_c_lo")
        projected, updated = sem("o_projected"), sem("o_updated")
        stats_ready, mom_ready, veps_ready, rstd_ready = sem("o_stats_ready"), sem("o_mom_ready"), sem("o_veps_ready"), sem("o_rstd_ready")
        normed, hi_done, lo_done, xposed = sem("o_normed"), sem("o_hi_done"), sem("o_lo_done"), sem("o_xposed")
        even_copied, odd_copied = sem("o_even_copied"), sem("o_odd_copied")
        stored = sem("o_stored")

        with nc.Block() as block:
            @block.sync
            def _(sp):
                def load(b):
                    if b >= 2:
                        sp.wait_ge(c_lo, (b - 1) * KC)
                    for r in range(3):
                        sp.dma_start(parts[:, b % 2, r, :, :], parts_v[b, r]).then_inc(parts_loaded[b % 2], 16)
                sp.dma_start(bob[:, :], bo.rearrange("(o n) -> o n", o=1).to_broadcast([P, D])).then_inc(consts_loaded, 16)
                sp.dma_start(bias[:, :], bv.rearrange("(c p) -> p c", p=P),
                             allow_slow_non_contiguous=True).then_inc(consts_loaded, 16)
                load(0)
                load(1)
                for b in range(B):
                    if b + 2 < B:
                        load(b + 2)
                    sp.wait_ge(updated, (b + 1) * QD)
                    sp.dma_start(x3_dram[b * S:(b + 1) * S, :].rearrange("(u p) d -> p u d", p=P),
                                 xres[:, b * QD:(b + 1) * QD, :]).then_inc(stored, 16)
                sp.wait_ge(stored, 16 * B)

            @block.gpsimd
            def _(pool):
                nc.gpsimd.memset(half[:, :], -0.5).then_inc(half_set, 1)
                pool.wait_ge(bo_gated, 1)
                for t in range(NT):
                    nc.gpsimd.tensor_tensor(xres[:, t, :], xres[:, t, :], bob[:, :], ALU.add).then_inc(biased, 1)
                pool.wait_ge(half_set, 1)
                for b in range(B):
                    q = slice(b * QD, (b + 1) * QD)
                    pool.wait_ge(veps_ready, b + 1)
                    nc.gpsimd.tensor_tensor(rstd[:, q], veps[:, q], half[:, q], ALU.pow).then_inc(rstd_ready, 1)

            @block.scalar
            def _(act):
                def high(b):
                    act.wait_ge(divided, b + 1)
                    if b >= 2:
                        act.wait_ge(projected, (b - 1) * QD)
                    for k in range(KC):
                        nc.scalar.activation(cpair[:, b % 2, 0, k, :], parts[:, b % 2, 0, k, :], ACT.Identity,
                                             bias=bias[:, k:k + 1]).then_inc(c_hi, 1)

                def x_high(b):
                    for t in range(b * QD, (b + 1) * QD):
                        act.wait_ge(normed, t + 1)
                        if t >= 4:
                            act.wait_ge(xposed, t - 3)
                        nc.scalar.copy(xpair[:, t % 4, 0, :], xn[:, t % 4, :]).then_inc(hi_done, 1)

                def x_copy(b):
                    for t in range(b * QD, (b + 1) * QD, 2):
                        act.wait_ge(xposed, t + 1)
                        nc.scalar.copy(xe_v[:, t % QD, b, :, :, :],
                                       psX[:, 0, :, :].rearrange("p r (e s) -> p r e s", s=PER)).then_inc(even_copied, 1)

                act.wait_ge(consts_loaded, 32)
                high(0)
                high(1)
                for b in range(B):
                    x_high(b)
                    if b + 2 < B:
                        high(b + 2)
                    x_copy(b)

            @block.vector
            def _(dve):
                def divide(b):
                    dve.wait_ge(parts_loaded[b % 2], 48 * (b // 2 + 1))
                    p = parts[:, b % 2, :, :, :].rearrange("p r c s -> p r (c s)")
                    nc.vector.reciprocal(p[:, 2, :], p[:, 2, :]).then_inc(rsum_ready, 1)
                    nc.vector.tensor_tensor(p[:, 0, :], p[:, 0, :], p[:, 1, :], ALU.add).then_inc(summed, 1)
                    dve.wait_ge(rsum_ready, b + 1)
                    dve.wait_ge(summed, b + 1)
                    nc.vector.tensor_tensor(p[:, 0, :], p[:, 0, :], p[:, 2, :], ALU.mult).then_inc(divided, 1)
                    for k in range(KC):
                        dve.wait_ge(c_hi, b * KC + k + 1)
                        nc.vector.scalar_tensor_tensor(cpair[:, b % 2, 1, k, :], parts[:, b % 2, 0, k, :], bias[:, k:k + 1],
                                                       cpair[:, b % 2, 0, k, :], ALU.add, ALU.subtract).then_inc(c_lo, 1)

                def update(b):
                    for t in range(b * QD, (b + 1) * QD):
                        dve.wait_ge(projected, t + 1)
                        dve.wait_ge(biased, t + 1)
                        nc.vector.scalar_tensor_tensor(xres[:, t, :], psG[:, t % 4, :], gates[:, 1:2], xres[:, t, :],
                                                       ALU.mult, ALU.add).then_inc(updated, 1)
                        dve.wait_ge(updated, t + 1)
                        nc.vector.bn_stats(stats[:, t, :], xres[:, t, :]).then_inc(stats_ready, 1)
                    for t in range(b * QD, (b + 1) * QD):
                        dve.wait_ge(stats_ready, t + 1)
                        nc.vector.bn_aggr(mom[:, t, :], stats[:, t, :]).then_inc(mom_ready, 1)
                    dve.wait_ge(mom_ready, (b + 1) * QD)
                    q = slice(b * QD, (b + 1) * QD)
                    nc.vector.tensor_scalar(veps[:, q], mom[:, q, 1], EPS, None, ALU.add).then_inc(veps_ready, 1)

                def normalise(b):
                    dve.wait_ge(rstd_ready, b + 1)
                    for t in range(b * QD, (b + 1) * QD):
                        if t >= 4:
                            dve.wait_ge(lo_done, t - 3)
                        nc.vector.tensor_scalar(xn[:, t % 4, :], xres[:, t, :], mom[:, t, 0:1], rstd[:, t:t + 1],
                                                ALU.subtract, ALU.mult).then_inc(normed, 1)

                def x_low(b):
                    for t in range(b * QD, (b + 1) * QD):
                        dve.wait_ge(hi_done, t + 1)
                        nc.vector.tensor_tensor(xpair[:, t % 4, 1, :], xn[:, t % 4, :], xpair[:, t % 4, 0, :],
                                                ALU.subtract).then_inc(lo_done, 1)

                def x_copy(b):
                    for t in range(b * QD + 1, (b + 1) * QD, 2):
                        dve.wait_ge(xposed, t + 1)
                        nc.vector.tensor_copy(xe_v[:, t % QD, b, :, :, :],
                                              psX[:, 1, :, :].rearrange("p r (e s) -> p r e s", s=PER)).then_inc(odd_copied, 1)

                dve.wait_ge(consts_loaded, 32)
                nc.vector.tensor_scalar(bob[:, :], bob[:, :], gates[:, 1:2], None, ALU.mult).then_inc(bo_gated, 1)
                divide(0)
                divide(1)
                for b in range(B):
                    update(b)
                    normalise(b)
                    x_low(b)
                    if b + 2 < B:
                        divide(b + 2)
                    x_copy(b)

            @block.tensor
            def _(pe):
                def project(b):
                    pe.wait_ge(c_lo, (b + 1) * KC)
                    for t in range(b * QD, (b + 1) * QD):
                        if t >= 4:
                            pe.wait_ge(updated, t - 3)
                        n = 0
                        for ra, rb in ((0, 0), (0, 1), (1, 0)):
                            for k in range(KC):
                                last = nc.tensor.matmul(psG[:, t % 4, :], cpair[:, b % 2, ra, k, t % QD * P:(t % QD + 1) * P],
                                                        woT[:, rb * KC + k, :], start=(n == 0), stop=(n == 3 * KC - 1))
                                n += 1
                        last.then_inc(projected, 1)

                def transposes(b):
                    for t in range(b * QD, (b + 1) * QD):
                        pe.wait_ge(lo_done, t + 1)
                        if t >= 2:
                            pe.wait_ge((even_copied, odd_copied)[t % 2], t // 2)
                        for r in range(2):
                            for k in range(KC):
                                last = nc.tensor.transpose(psX[:, t % 2, r * KC + k, :], xpair[:, t % 4, r, k * P:(k + 1) * P],
                                                           ident[:, :])
                        last.then_inc(xposed, 1)

                project(0)
                for b in range(B):
                    if b + 1 < B:
                        project(b + 1)
                    transposes(b)


def expert_phase(nc, w1, b1, w2, b2, ident, x3_dram, gates, xeT, out):
    F = w1.shape[2]
    FC = F // P
    PER = S // E
    NTOK = B * PER
    w1_v = w1.rearrange("e (k p) f -> e k p f", p=P)
    w2_v = w2.rearrange("e (k c p) d -> e k p c d", c=FC // 4, p=P)
    x3_v = x3_dram.rearrange("(b e s) d -> e b s d", b=B, e=E)
    out_v = out.rearrange("b (e s) d -> e b s d", e=E)
    with ExitStack() as c:
        sb = lambda name, shape, dt: c.enter_context(nc.sbuf_tensor(name, shape, dt))
        sem = lambda name: c.enter_context(nc.semaphore(name))
        piece = sb("e_piece", [P, 4, F], F32)
        w1p = sb("e_w1p", [P, 2, KC, F], BF16)
        w2p = sb("e_w2p", [P, 2, FC, D], BF16)
        b1rows = sb("e_b1rows", [P, P], F32)
        identf = sb("e_identf", [P, P], F32)
        b1T = sb("e_b1T", [P, E * FC], F32)
        g32 = sb("e_g32", [P, 2, 2, NTOK], F32)
        hT = sb("e_hT", [P, 2, FC, NTOK], BF16)
        x3 = sb("e_x3", [P, 2, D], F32)
        b2b = sb("e_b2b", [P, D], F32)
        base = sb("e_base", [P, 2, D], F32)
        outs = sb("e_outs", [P, 2, D], F32)
        psG = c.enter_context(nc.psum_tensor("e_psG", [P, 4, 2, NTOK], F32))
        psO = c.enter_context(nc.psum_tensor("e_psO", [P, 2, D], F32))
        psB = c.enter_context(nc.psum_tensor("e_psB", [P, P], F32))
        b1_loaded, identf_ready, b1_xposed, b1_ready = sem("e_b1_loaded"), sem("e_identf_ready"), sem("e_b1_xposed"), sem("e_b1_ready")
        loaded = [sem(f"e_loaded{i}") for i in range(4)]
        x_loaded = sem("e_x_loaded")
        w_hi, w_lo = sem("e_w_hi"), sem("e_w_lo")
        lifted = sem("e_lifted")
        gelu_done, h_hi, h_lo = sem("e_gelu_done"), sem("e_h_hi"), sem("e_h_lo")
        based, updated = sem("e_based"), sem("e_updated")
        lowered = sem("e_lowered")
        stored = sem("e_stored")

        with nc.Block() as block:
            @block.sync
            def _(sp):
                def load(e, p):
                    ee = bass.ds(e, 1)
                    sp.wait_ge(w_lo, e * 8 + p + 1)
                    if p < 4:
                        sp.dma_start(piece[:, p, :], w1_v[ee, p].rearrange("o p f -> p (o f)")).then_inc(loaded[p], 16)
                    else:
                        sp.dma_start(piece[:, p - 4, :].rearrange("p (c d) -> p c d", d=D),
                                     w2_v[ee, p - 4].rearrange("o p c d -> p (o c) d")).then_inc(loaded[p - 4], 16)

                def load_x(e):
                    ee = bass.ds(e, 1)
                    sp.wait_ge(based, e * 2 + 2)
                    for m in range(2):
                        sp.dma_start(x3[:, m, :], x3_v[ee, 2 * m:2 * m + 2].rearrange("o b s d -> (o b) s d")).then_inc(x_loaded, 16)
                    sp.dma_start(b2b[:, :], b2[ee, :].to_broadcast([P, D])).then_inc(x_loaded, 16)

                def store(e):
                    sp.wait_ge(updated, e * 2 + 4)
                    for m in range(2):
                        sp.dma_start(out_v[bass.ds(e, 1), 2 * m:2 * m + 2].rearrange("o b s d -> (o b) s d"),
                                     outs[:, m, :]).then_inc(stored, 16)

                def expert(e, more):
                    for p in range(4, 8):
                        load(e, p)
                    if more:
                        for p in range(4):
                            load(e + 1, p)
                    store(e)
                    if more:
                        load_x(e + 1)

                sp.sem_inc(stored, 32)
                sp.dma_start(b1rows[:, :], b1.rearrange("e (c f) -> (e c) f", f=P)).then_inc(b1_loaded, 16)
                for p in range(4):
                    load(0, p)
                load_x(0)
                with sp.Fori(0, E - 1) as e:
                    expert(e, True)
                expert(E - 1, False)
                sp.wait_ge(stored, 32 * (E + 1))

            @block.scalar
            def _(act):
                def weights(e, p):
                    act.wait_ge(loaded[p % 4], e * 32 + p // 4 * 16 + 16)
                    if p < 4:
                        act.wait_ge(lifted, e * 8 + 8)
                        nc.scalar.copy(w1p[:, 0, p, :], piece[:, p, :]).then_inc(w_hi, 1)
                    else:
                        act.wait_ge(lowered, e * 2 + 2)
                        nc.scalar.copy(w2p[:, 0, (p - 4) * 4:(p - 3) * 4, :],
                                       piece[:, p - 4, :].rearrange("p (c d) -> p c d", d=D)).then_inc(w_hi, 1)

                def expert(e, more):
                    for g in range(FC // 2):
                        act.wait_ge(lifted, e * 8 + g + 9)
                        act.wait_ge(h_lo, e * 8 + g + 3)
                        for i in range(2):
                            nc.scalar.activation(g32[:, g % 2, i, :], psG[:, g % 4, i, :], ACT.Gelu,
                                                 bias=b1T[:, bass.ds(e * FC + 2 * g + i, 1)]).then_inc(gelu_done, 1)
                        act.wait_ge(gelu_done, e * FC + 2 * g + 2)
                        nc.scalar.copy(hT[:, 0, 2 * g:2 * g + 2, :], g32[:, g % 2, :, :]).then_inc(h_hi, 1)
                        if g % 2 == 1:
                            weights(e, 4 + g // 2)
                    if more:
                        for p in range(4):
                            weights(e + 1, p)

                act.sem_inc(lifted, 8)
                nc.scalar.copy(identf[:, :], ident[:, :]).then_inc(identf_ready, 1)
                act.wait_ge(b1_xposed, 1)
                nc.scalar.copy(b1T[:, :], psB[:, :]).then_inc(b1_ready, 1)
                for p in range(4):
                    weights(0, p)
                act.wait_ge(b1_ready, 1)
                with act.Fori(0, E - 1) as e:
                    expert(e, True)
                expert(E - 1, False)

            @block.vector
            def _(dve):
                def weights(e, p):
                    dve.wait_ge(w_hi, e * 8 + p + 1)
                    if p < 4:
                        nc.vector.tensor_tensor(w1p[:, 1, p, :], piece[:, p, :], w1p[:, 0, p, :], ALU.subtract).then_inc(w_lo, 1)
                    else:
                        nc.vector.tensor_tensor(w2p[:, 1, (p - 4) * 4:(p - 3) * 4, :],
                                                piece[:, p - 4, :].rearrange("p (c d) -> p c d", d=D),
                                                w2p[:, 0, (p - 4) * 4:(p - 3) * 4, :], ALU.subtract).then_inc(w_lo, 1)

                def expert(e, more):
                    for g in range(FC // 2):
                        dve.wait_ge(h_hi, e * 8 + g + 1)
                        nc.vector.tensor_tensor(hT[:, 1, 2 * g:2 * g + 2, :], g32[:, g % 2, :, :], hT[:, 0, 2 * g:2 * g + 2, :],
                                                ALU.subtract).then_inc(h_lo, 1)
                        if g % 2 == 1:
                            weights(e, 4 + g // 2)
                    dve.wait_ge(x_loaded, e * 48 + 48)
                    for m in range(2):
                        dve.wait_ge(updated, e * 2 + m + 1)
                        nc.vector.scalar_tensor_tensor(base[:, m, :], b2b[:, :], gates[:, 3:4], x3[:, m, :],
                                                       ALU.mult, ALU.add).then_inc(based, 1)
                    if more:
                        for p in range(4):
                            weights(e + 1, p)
                    dve.wait_ge(stored, e * 32 + 32)
                    for m in range(2):
                        dve.wait_ge(lowered, e * 2 + m + 3)
                        dve.wait_ge(based, e * 2 + m + 3)
                        nc.vector.scalar_tensor_tensor(outs[:, m, :], psO[:, m, :], gates[:, 3:4], base[:, m, :],
                                                       ALU.mult, ALU.add).then_inc(updated, 1)

                for s, n in ((w_lo, 4), (h_lo, 4), (based, 2), (updated, 2)):
                    dve.sem_inc(s, n)
                for p in range(4):
                    weights(0, p)
                with dve.Fori(0, E - 1) as e:
                    expert(e, True)
                expert(E - 1, False)

            @block.tensor
            def _(pe):
                def expert(e):
                    ee = bass.ds(e, 1)
                    pe.wait_ge(w_lo, e * 8 + 8)
                    for g in range(FC // 2):
                        pe.wait_ge(h_lo, e * 8 + g + 1)
                        for i in range(2):
                            f = (2 * g + i) * P
                            n = 0
                            for ra, rb in ((0, 0), (0, 1), (1, 0)):
                                for k in range(KC):
                                    last = nc.tensor.matmul(psG[:, g % 4, i, :], w1p[:, ra, k, f:f + P],
                                                            xeT[:, rb * KC + k, ee, :].rearrange("p o s -> p (o s)"),
                                                            start=(n == 0), stop=(n == 3 * KC - 1))
                                    n += 1
                        last.then_inc(lifted, 1)
                    for m in range(2):
                        pe.wait_ge(updated, e * 2 + m + 1)
                        for k in range(FC):
                            if m == 0 and k % 2 == 0:
                                pe.wait_ge(h_lo, e * 8 + k // 2 + 5)
                            if m == 0 and k % 4 == 0:
                                pe.wait_ge(w_lo, e * 8 + k // 4 + 9)
                            for i, (ra, rb) in enumerate(((0, 0), (0, 1), (1, 0))):
                                last = nc.tensor.matmul(psO[:, m, :], hT[:, ra, k, m * P:(m + 1) * P], w2p[:, rb, k, :],
                                                        start=(k == 0 and i == 0), stop=(k == FC - 1 and i == 2))
                        last.then_inc(lowered, 1)

                pe.sem_inc(lowered, 2)
                pe.wait_ge(b1_loaded, 16)
                pe.wait_ge(identf_ready, 1)
                nc.tensor.transpose(psB[:, :], b1rows[:, :], identf[:, :]).then_inc(b1_xposed, 1)
                with pe.Fori(0, E - 1) as e:
                    expert(e)
                expert(E - 1)


def flamingo_kernel(nc, a, out):
    dram = lambda name, shape, dt: nc.dram_tensor(name, shape, dt, kind="Internal").ap()
    keys_dram = dram("keys", (B * 2, 2, D, T // 2), BF16)
    queries_dram = dram("queries", (B, 2, D, S), BF16)
    mixed_dram = dram("mixed", (B, 3, D, S), F32)
    dispatch_dram = dram("dispatch", ((NT + E - 1) * P, DW // 2), F32)
    mixture_dram = dram("mixture", ((NT + E - 1) * P, D), F32)
    x3_dram = dram("x3", (NT * P, D), F32)
    values_dram = dram("values", (B, T, NH * VW), BF16)
    used = []

    def sem(name):
        used.append(nc.alloc_semaphore(name))
        return used[-1]

    with ExitStack() as c:
        ident = c.enter_context(nc.sbuf_tensor("ident", [P, P], BF16))
        xres = c.enter_context(nc.sbuf_tensor("xres", [P, NT, D], F32))
        moments = c.enter_context(nc.sbuf_tensor("moments", [P, NT, 2], F32))
        gates = c.enter_context(nc.sbuf_tensor("gates", [P, 4], F32))
        with ExitStack() as early:
            ctxN = early.enter_context(nc.sbuf_tensor("ctxN", [P, B * T // P, 2, D], BF16))
            ctxT = early.enter_context(nc.sbuf_tensor("ctxT", [P, 2 * KC, B * T], BF16))
            context_phase(nc, sem, a["ctx_2048"], a["L1_xattn_Wk"], a["L1_xattn_bk"], a["L1_xattn_Wv"],
                          keys_dram, values_dram, ident, ctxN, ctxT, a["x"], xres, moments,
                          a["g_xattn"], a["g_ffn"], gates)
            readout_phase(nc, sem, a["mask_BxS2_bk0"], gates, ident, ctxN, ctxT, xres, moments)
        with ExitStack() as moe:
            wT = moe.enter_context(nc.sbuf_tensor("wT", [P, E, 3, KC, D], BF16))
            scales = moe.enter_context(nc.sbuf_tensor("scales", [P, 2, NT + E - 1], F32))
            expert_of = moe.enter_context(nc.sbuf_tensor("expert_of", [P, NT + E - 1], mybir.dt.int32))
            place = moe.enter_context(nc.sbuf_tensor("place", [P, NT], mybir.dt.int32))
            router_phase(nc, sem, a["L0_ffn_router_w"], (a["L0_ffn_wg"], a["L0_ffn_wu"], a["L0_ffn_wd"]), ident, xres, moments,
                         wT, scales, expert_of, place, dispatch_dram)
            mixture_phase(nc, sem, ident, wT, scales, expert_of, dispatch_dram, mixture_dram)
            gather_phase(nc, sem, place, gates, mixture_dram, xres, moments)
        nc.clear_and_free_semaphores(used)
        nc.all_engine_barrier()
        with ExitStack() as late:
            woT = late.enter_context(nc.sbuf_tensor("woT", [P, 2 * KC, D], BF16))
            query_phase(nc, a["L1_xattn_Wq"], a["L1_xattn_bq"], a["L1_xattn_Wo"], queries_dram, ident, xres, moments, woT)
            attention_phase(nc, queries_dram, keys_dram, values_dram, mixed_dram, ident)
            xeT = late.enter_context(nc.sbuf_tensor("xeT", [P, 2 * KC, E, B * S // E], BF16))
            output_phase(nc, mixed_dram, a["L1_xattn_bv"], a["L1_xattn_bo"], ident, xres, woT,
                         x3_dram, gates, xeT)
            expert_phase(nc, a["L1_ffn_w1"], a["L1_ffn_b1"], a["L1_ffn_w2"], a["L1_ffn_b2"], ident, x3_dram, gates, xeT, out)


_INS = ['x', 'ctx_2048', 'mask_BxS2_bk0', 'g_xattn', 'g_ffn', 'L0_ffn_router_w', 'L0_ffn_wg', 'L0_ffn_wu',
        'L0_ffn_wd', 'L1_xattn_Wq', 'L1_xattn_bq', 'L1_xattn_Wk', 'L1_xattn_bk', 'L1_xattn_Wv', 'L1_xattn_bv',
        'L1_xattn_Wo', 'L1_xattn_bo', 'L1_ffn_w1', 'L1_ffn_b1', 'L1_ffn_w2', 'L1_ffn_b2']


def kernel(**inputs):
    import numpy as np
    import concourse.bacc as bacc
    from concourse import mybir as my
    from concourse.bass_utils import run_bass_kernel_spmd

    nc = bacc.Bacc("TRN2", target_bir_lowering=False, num_devices=1)
    arrays, aps = {}, {}
    for name in _INS:
        a = np.ascontiguousarray(inputs[name])
        arrays["in_" + name] = a
        aps[name] = nc.dram_tensor("in_" + name, a.shape, my.dt.from_np(a.dtype), kind="ExternalInput").ap()
    out = nc.dram_tensor("out_0", (4, 512, 512), my.dt.float32, kind="ExternalOutput").ap()
    flamingo_kernel(nc, aps, out)
    r = run_bass_kernel_spmd(nc, [arrays], core_ids=[0])
    return r.results[0]["out_0"]
```
